# Optimizing a Trainium2 kernel written in Bass

```python
import numpy as np
import jax
import jax.numpy as jnp

def _softmax(x, axis=-1):
    return jax.nn.softmax(x, axis=axis)

def _gelu(x):
    return jax.nn.gelu(x, approximate=True)

def _silu(x):
    return jax.nn.silu(x)

def _sigmoid(x):
    return jax.nn.sigmoid(x)

def _layernorm(x, axis=-1, eps=1e-05):
    m = jnp.mean(x, axis=axis, keepdims=True)
    v = jnp.var(x, axis=axis, keepdims=True)
    return (x - m) / jnp.sqrt(v + eps)

def _scatter_add(tgt, idx, src, axis=0):
    return tgt.at[idx].add(src)

def _segment_sum(src, seg, n):
    return jax.ops.segment_sum(src, seg, n)
kernel_name = 'mk_seq_postln_d2_jaxref_r8_e7913c'

def setup_inputs(seed: int=0):
    np.random.seed(seed)
    _w = jnp.asarray

    def _L0_attn_setup():
        import jax, jax.numpy as jnp
        import numpy as np
        B, S, D = (4, 512, 128)
        H = 8
        DK = D // H
        DV = D // H
        KLEPE = 5
        ROPE_BASE = 10000.0

        def rotate_half(x):
            x1, x2 = jnp.split(x, 2, axis=-1)
            return jnp.concatenate([-x2, x1], axis=-1)

        def rope_sin_cos(seq_len, dim):
            inv_freq = 1.0 / ROPE_BASE ** (jnp.arange(0, dim, 2, dtype=jnp.float32) / dim)
            freqs = jnp.arange(seq_len, dtype=jnp.float32)[:, None] * inv_freq[None, :]
            emb = jnp.concatenate([freqs, freqs], axis=-1)
            return (jnp.sin(emb), jnp.cos(emb))

        def mala_attn(q, k, v):
            sin, cos = rope_sin_cos(q.shape[1], q.shape[-1])
            sin, cos = (sin[None, :, None, :], cos[None, :, None, :])
            q = q * cos + rotate_half(q) * sin
            k = k * cos + rotate_half(k) * sin
            scale = q.shape[-1] ** (-0.5)
            seq_len = q.shape[1]
            kv = jnp.einsum('bshd,bshe->bhde', k, v)
            ksum = k.sum(axis=1)
            vsum = v.sum(axis=1)
            num = jnp.einsum('bshd,bhde->bshe', q, kv) * scale + vsum[:, None, :, :]
            den = jnp.einsum('bshd,bhd->bsh', q, ksum) * scale + seq_len
            return num / den[..., None]

        def lepe_conv(v, w, b):
            Bb, Ss = (v.shape[0], v.shape[1])
            x = v.transpose(0, 2, 3, 1).reshape(Bb, H * DV, Ss)
            y = jax.lax.conv_general_dilated(x, w, window_strides=(1,), padding=[(KLEPE // 2, KLEPE // 2)], dimension_numbers=('NCH', 'OIH', 'NCH'), feature_group_count=H * DV)
            y = y + b[None, :, None]
            return y.reshape(Bb, H, DV, Ss).transpose(0, 3, 1, 2)
        key = jax.random.key(seed)
        ks = jax.random.split(key, 8)
        w = 0.02
        return {'hidden_states': jax.random.normal(ks[0], (B, S, D), dtype=jnp.float32), 'Wq': jax.random.normal(ks[1], (D, D), dtype=jnp.float32) * w, 'Wk': jax.random.normal(ks[2], (D, D), dtype=jnp.float32) * w, 'Wv': jax.random.normal(ks[3], (D, D), dtype=jnp.float32) * w, 'Wg': jax.random.normal(ks[4], (D, D), dtype=jnp.float32) * w, 'Wo': jax.random.normal(ks[5], (D, D), dtype=jnp.float32) * w, 'lepe_w': jax.random.normal(ks[6], (D, 1, KLEPE), dtype=jnp.float32) * 0.1, 'lepe_b': jnp.zeros((D,), dtype=jnp.float32)}
    _L0_attn_in = _L0_attn_setup()

    def _L0_ffn_setup():
        import jax, jax.numpy as jnp
        import numpy as np
        B, C, D, O = (4, 512, 128, 128)
        PROJ = 32
        RANKS = [1, 2, 4, 8]
        E = len(RANKS)
        CLAMP_MAX = float(np.log(1.0 / 0.01))

        def _l2norm(v, axis):
            return v / jnp.maximum(jnp.linalg.norm(v, axis=axis, keepdims=True), 1e-12)
        key = jax.random.key(seed)
        ks = jax.random.split(key, 16)
        inp = {'x': jax.random.normal(ks[0], (B, C, D), dtype=jnp.float32), 'W': jax.random.normal(ks[1], (O, D), dtype=jnp.float32) / np.sqrt(D), 'Wp': jax.random.normal(ks[2], (PROJ, D), dtype=jnp.float32) / np.sqrt(D), 'bp': jnp.zeros((PROJ,), dtype=jnp.float32), 'sim': jax.random.normal(ks[3], (PROJ, E), dtype=jnp.float32) * 0.01, 'temp': jnp.full((1,), np.log(1.0 / 0.5), dtype=jnp.float32)}
        for i, r in enumerate(RANKS):
            inp[f'Wd{i}'] = jax.random.normal(ks[4 + 2 * i], (r, D), dtype=jnp.float32) / r
            inp[f'Wu{i}'] = jax.random.normal(ks[5 + 2 * i], (O, r), dtype=jnp.float32) * 0.01
        return inp
    _L0_ffn_in = _L0_ffn_setup()

    def _L1_attn_setup():
        import jax, jax.numpy as jnp
        import numpy as np
        import math
        DK = 128
        key = jax.random.key(seed)
        k1, k2 = jax.random.split(key)
        x = jax.random.normal(k1, (4, 256, 128), dtype=jnp.float32)
        W = jax.random.normal(k2, (128, 3 * DK), dtype=jnp.float32) * (1.0 / math.sqrt(128))
        b = jnp.zeros((3 * DK,), dtype=jnp.float32)
        return {'x': x, 'W': W, 'b': b}
    _L1_attn_in = _L1_attn_setup()

    def _L1_ffn_setup():
        import jax, jax.numpy as jnp
        import numpy as np
        B, S, H = (2, 128, 128)
        E, F = (16, 64)
        G, TOPK_G, TOPK = (4, 2, 4)
        N_SHARED = 2
        ROUTE_SCALE = 1.0
        FS = N_SHARED * F

        def _gate(x, w_gate):
            T = x.shape[0]
            scores = jax.nn.sigmoid(x @ w_gate.T)
            sv = scores.reshape(T, G, E // G)
            group_scores = jax.lax.top_k(sv, 2)[0].sum(-1)
            top_groups = jax.lax.top_k(group_scores, TOPK_G)[1]
            allowed = jnp.zeros((T, G), dtype=bool).at[jnp.arange(T)[:, None], top_groups].set(True)
            masked = jnp.where(allowed[:, :, None], sv, -jnp.inf).reshape(T, E)
            _, idx = jax.lax.top_k(masked, TOPK)
            w = jnp.take_along_axis(scores, idx, axis=1)
            w = w / (w.sum(-1, keepdims=True) + 1e-06) * ROUTE_SCALE
            return (w, idx)

        def _swiglu(x, w1, w3, w2):
            return jax.nn.silu(x @ w1.T) * (x @ w3.T) @ w2.T
        key = jax.random.key(seed)
        ks = jax.random.split(key, 8)
        scale = 0.02
        return {'hidden_states': jax.random.normal(ks[0], (B, S, H), dtype=jnp.float32), 'w_gate': jax.random.normal(ks[1], (E, H), dtype=jnp.float32) * scale, 'w1_e': jax.random.normal(ks[2], (E, F, H), dtype=jnp.float32) * scale, 'w3_e': jax.random.normal(ks[3], (E, F, H), dtype=jnp.float32) * scale, 'w2_e': jax.random.normal(ks[4], (E, H, F), dtype=jnp.float32) * scale, 'w1_s': jax.random.normal(ks[5], (FS, H), dtype=jnp.float32) * scale, 'w3_s': jax.random.normal(ks[6], (FS, H), dtype=jnp.float32) * scale, 'w2_s': jax.random.normal(ks[7], (H, FS), dtype=jnp.float32) * scale}
    _L1_ffn_in = _L1_ffn_setup()
    _d = {'L0_attn_hidden_states': _L0_attn_in['hidden_states'], 'L0_attn_Wq': _L0_attn_in['Wq'], 'L0_attn_Wk': _L0_attn_in['Wk'], 'L0_attn_Wv': _L0_attn_in['Wv'], 'L0_attn_Wg': _L0_attn_in['Wg'], 'L0_attn_Wo': _L0_attn_in['Wo'], 'L0_attn_lepe_w': _L0_attn_in['lepe_w'], 'L0_attn_lepe_b': _L0_attn_in['lepe_b'], 'L0_ffn_W': _L0_ffn_in['W'], 'L0_ffn_Wp': _L0_ffn_in['Wp'], 'L0_ffn_bp': _L0_ffn_in['bp'], 'L0_ffn_sim': _L0_ffn_in['sim'], 'L0_ffn_temp': _L0_ffn_in['temp'], 'L0_ffn_Wd0': _L0_ffn_in['Wd0'], 'L0_ffn_Wu0': _L0_ffn_in['Wu0'], 'L0_ffn_Wd1': _L0_ffn_in['Wd1'], 'L0_ffn_Wu1': _L0_ffn_in['Wu1'], 'L0_ffn_Wd2': _L0_ffn_in['Wd2'], 'L0_ffn_Wu2': _L0_ffn_in['Wu2'], 'L0_ffn_Wd3': _L0_ffn_in['Wd3'], 'L0_ffn_Wu3': _L0_ffn_in['Wu3'], 'L1_attn_W': _L1_attn_in['W'], 'L1_attn_b': _L1_attn_in['b'], 'L1_ffn_w_gate': _L1_ffn_in['w_gate'], 'L1_ffn_w1_e': _L1_ffn_in['w1_e'], 'L1_ffn_w3_e': _L1_ffn_in['w3_e'], 'L1_ffn_w2_e': _L1_ffn_in['w2_e'], 'L1_ffn_w1_s': _L1_ffn_in['w1_s'], 'L1_ffn_w3_s': _L1_ffn_in['w3_s'], 'L1_ffn_w2_s': _L1_ffn_in['w2_s']}
    _x0 = _d['L0_attn_hidden_states']
    _d['L0_attn_hidden_states'] = jax.random.normal(jax.random.fold_in(jax.random.key(seed), 1), (32, 256, 128), dtype=_x0.dtype)
    del _x0
    return _d

def reference(L0_attn_hidden_states, L0_attn_Wq, L0_attn_Wk, L0_attn_Wv, L0_attn_Wg, L0_attn_Wo, L0_attn_lepe_w, L0_attn_lepe_b, L0_ffn_W, L0_ffn_Wp, L0_ffn_bp, L0_ffn_sim, L0_ffn_temp, L0_ffn_Wd0, L0_ffn_Wu0, L0_ffn_Wd1, L0_ffn_Wu1, L0_ffn_Wd2, L0_ffn_Wu2, L0_ffn_Wd3, L0_ffn_Wu3, L1_attn_W, L1_attn_b, L1_ffn_w_gate, L1_ffn_w1_e, L1_ffn_w3_e, L1_ffn_w2_e, L1_ffn_w1_s, L1_ffn_w3_s, L1_ffn_w2_s):

    def _L0_attn_ref(hidden_states, Wq, Wk, Wv, Wg, Wo, lepe_w, lepe_b):
        import jax, jax.numpy as jnp
        import numpy as np
        B, S, D = (4, 512, 128)
        H = 8
        DK = D // H
        DV = D // H
        KLEPE = 5
        ROPE_BASE = 10000.0

        def rotate_half(x):
            x1, x2 = jnp.split(x, 2, axis=-1)
            return jnp.concatenate([-x2, x1], axis=-1)

        def rope_sin_cos(seq_len, dim):
            inv_freq = 1.0 / ROPE_BASE ** (jnp.arange(0, dim, 2, dtype=jnp.float32) / dim)
            freqs = jnp.arange(seq_len, dtype=jnp.float32)[:, None] * inv_freq[None, :]
            emb = jnp.concatenate([freqs, freqs], axis=-1)
            return (jnp.sin(emb), jnp.cos(emb))

        def mala_attn(q, k, v):
            sin, cos = rope_sin_cos(q.shape[1], q.shape[-1])
            sin, cos = (sin[None, :, None, :], cos[None, :, None, :])
            q = q * cos + rotate_half(q) * sin
            k = k * cos + rotate_half(k) * sin
            scale = q.shape[-1] ** (-0.5)
            seq_len = q.shape[1]
            kv = jnp.einsum('bshd,bshe->bhde', k, v)
            ksum = k.sum(axis=1)
            vsum = v.sum(axis=1)
            num = jnp.einsum('bshd,bhde->bshe', q, kv) * scale + vsum[:, None, :, :]
            den = jnp.einsum('bshd,bhd->bsh', q, ksum) * scale + seq_len
            return num / den[..., None]

        def lepe_conv(v, w, b):
            Bb, Ss = (v.shape[0], v.shape[1])
            x = v.transpose(0, 2, 3, 1).reshape(Bb, H * DV, Ss)
            y = jax.lax.conv_general_dilated(x, w, window_strides=(1,), padding=[(KLEPE // 2, KLEPE // 2)], dimension_numbers=('NCH', 'OIH', 'NCH'), feature_group_count=H * DV)
            y = y + b[None, :, None]
            return y.reshape(Bb, H, DV, Ss).transpose(0, 3, 1, 2)
        Bb, Ss, _ = hidden_states.shape
        q = (hidden_states @ Wq.T).reshape(Bb, Ss, H, DK)
        k = (hidden_states @ Wk.T).reshape(Bb, Ss, H, DK)
        v = (hidden_states @ Wv.T).reshape(Bb, Ss, H, DV)
        o_gate = hidden_states @ Wg.T
        o = mala_attn(q, k, v) + lepe_conv(v, lepe_w, lepe_b)
        o = o.reshape(Bb, Ss, H * DV) * o_gate
        return o @ Wo.T

    def _L0_ffn_ref(x, W, Wp, bp, sim, temp, Wd0, Wu0, Wd1, Wu1, Wd2, Wu2, Wd3, Wu3):
        import jax, jax.numpy as jnp
        import numpy as np
        B, C, D, O = (4, 512, 128, 128)
        PROJ = 32
        RANKS = [1, 2, 4, 8]
        E = len(RANKS)
        CLAMP_MAX = float(np.log(1.0 / 0.01))

        def _l2norm(v, axis):
            return v / jnp.maximum(jnp.linalg.norm(v, axis=axis, keepdims=True), 1e-12)
        base = jnp.einsum('bcd,od->bco', x, W)
        xf = x.reshape(-1, x.shape[-1])
        proj = _l2norm(xf @ Wp.T + bp, axis=1)
        simn = _l2norm(sim, axis=0)
        scale = jnp.exp(jnp.minimum(temp, CLAMP_MAX))
        logits = proj @ simn * scale
        lw = jax.nn.softmax(logits, axis=1)
        top1 = jnp.argmax(lw, axis=1)
        ret = jnp.where(jnp.arange(E)[None, :] == top1[:, None], lw, 0.0)
        ret = ret.reshape(x.shape[0], x.shape[1], E)
        downs = (Wd0, Wd1, Wd2, Wd3)
        ups = (Wu0, Wu1, Wu2, Wu3)
        l = jnp.stack([jnp.einsum('bcr,or->bco', jnp.einsum('bcd,rd->bcr', x, d), u) for d, u in zip(downs, ups)], axis=2)
        res = jnp.sum(ret[..., None] * l, axis=2)
        return base + res

    def _L1_attn_ref(x, W, b):
        import jax, jax.numpy as jnp
        import numpy as np
        import math
        DK = 128
        qkv = jnp.einsum('btc,cd->btd', x, W) + b
        q, k, v = jnp.split(qkv, 3, axis=-1)
        scale = 1.0 / math.sqrt(DK)
        weights = jnp.einsum('btc,bTc->btT', q, k) * scale
        T = weights.shape[-1]
        mask = jnp.tril(jnp.ones((T, T), dtype=jnp.float32))
        logits = jnp.where(mask == 0, jnp.float32(-9000000000000000.0), weights)
        attention = jax.nn.softmax(logits, axis=-1)
        values = jnp.einsum('btT,bTc->btc', attention, v)
        return values

    def _L1_ffn_ref(hidden_states, w_gate, w1_e, w3_e, w2_e, w1_s, w3_s, w2_s):
        import jax, jax.numpy as jnp
        import numpy as np
        B, S, H = (2, 128, 128)
        E, F = (16, 64)
        G, TOPK_G, TOPK = (4, 2, 4)
        N_SHARED = 2
        ROUTE_SCALE = 1.0
        FS = N_SHARED * F

        def _gate(x, w_gate):
            T = x.shape[0]
            scores = jax.nn.sigmoid(x @ w_gate.T)
            sv = scores.reshape(T, G, E // G)
            group_scores = jax.lax.top_k(sv, 2)[0].sum(-1)
            top_groups = jax.lax.top_k(group_scores, TOPK_G)[1]
            allowed = jnp.zeros((T, G), dtype=bool).at[jnp.arange(T)[:, None], top_groups].set(True)
            masked = jnp.where(allowed[:, :, None], sv, -jnp.inf).reshape(T, E)
            _, idx = jax.lax.top_k(masked, TOPK)
            w = jnp.take_along_axis(scores, idx, axis=1)
            w = w / (w.sum(-1, keepdims=True) + 1e-06) * ROUTE_SCALE
            return (w, idx)

        def _swiglu(x, w1, w3, w2):
            return jax.nn.silu(x @ w1.T) * (x @ w3.T) @ w2.T
        shape = hidden_states.shape
        x = hidden_states.reshape(-1, H)
        weights, idx = _gate(x, w_gate)
        combine = (jax.nn.one_hot(idx, E, dtype=x.dtype) * weights[..., None]).sum(1)
        g = jax.nn.silu(jnp.einsum('th,efh->tef', x, w1_e))
        u = jnp.einsum('th,efh->tef', x, w3_e)
        routed = jnp.einsum('tef,ehf,te->th', g * u, w2_e, combine)
        shared = _swiglu(x, w1_s, w3_s, w2_s)
        return (routed + shared).reshape(shape)
    x = L0_attn_hidden_states
    x = _layernorm(x + _L0_attn_ref(x, L0_attn_Wq, L0_attn_Wk, L0_attn_Wv, L0_attn_Wg, L0_attn_Wo, L0_attn_lepe_w, L0_attn_lepe_b), axis=-1)
    x = _layernorm(x + _L0_ffn_ref(x, L0_ffn_W, L0_ffn_Wp, L0_ffn_bp, L0_ffn_sim, L0_ffn_temp, L0_ffn_Wd0, L0_ffn_Wu0, L0_ffn_Wd1, L0_ffn_Wu1, L0_ffn_Wd2, L0_ffn_Wu2, L0_ffn_Wd3, L0_ffn_Wu3), axis=-1)
    x = _layernorm(x + _L1_attn_ref(x, L1_attn_W, L1_attn_b), axis=-1)
    x = _layernorm(x + _L1_ffn_ref(x, L1_ffn_w_gate, L1_ffn_w1_e, L1_ffn_w3_e, L1_ffn_w2_e, L1_ffn_w1_s, L1_ffn_w3_s, L1_ffn_w2_s), axis=-1)
    return x

_drawn_inputs = setup_inputs


def setup_inputs(seed=0):
    import zlib

    import numpy as np

    out = dict(_drawn_inputs(seed))
    spreads = {'L0_attn_lepe_b': (0.0, 0.8), 'L0_ffn_bp': (0.0, 0.8), 'L1_attn_b': (0.0, 0.1)}
    factors = {'L0_attn_Wq': 8.0,
     'L0_attn_Wk': 8.0,
     'L0_attn_Wv': 8.0,
     'L0_attn_Wg': 8.0,
     'L0_attn_Wo': 8.0,
     'L0_attn_lepe_w': 8.0,
     'L0_ffn_Wp': 3.003,
     'L0_ffn_sim': 2.899,
     'L0_ffn_Wd0': 3.374,
     'L0_ffn_Wu0': 3.2,
     'L0_ffn_Wd1': 5.492,
     'L0_ffn_Wu1': 5.453,
     'L0_ffn_Wd2': 7.785,
     'L0_ffn_Wu2': 7.667,
     'L0_ffn_Wd3': 8.0,
     'L0_ffn_Wu3': 8.0,
     'L1_ffn_w_gate': 8.0,
     'L1_ffn_w1_e': 8.0,
     'L1_ffn_w3_e': 8.0,
     'L1_ffn_w2_e': 8.0,
     'L1_ffn_w1_s': 8.0,
     'L1_ffn_w3_s': 8.0,
     'L1_ffn_w2_s': 8.0}
    for name, (base, spread) in spreads.items():
        noise = np.random.default_rng([zlib.crc32(name.encode()), seed]).standard_normal(out[name].shape)
        drawn = base * np.exp(spread * noise) if base else spread * noise
        out[name] = jnp.asarray(drawn.astype(out[name].dtype))
    for name, factor in factors.items():
        out[name] = (out[name] * factor).astype(out[name].dtype)
    return out
```

```python
from contextlib import ExitStack

import numpy as np

import concourse.bass as bass
from concourse import mybir

ALU = mybir.AluOpType
ACT = mybir.ActivationFunctionType
AX = mybir.AxisListType
F32 = mybir.dt.float32
F32R = mybir.dt.float32r
BF16 = mybir.dt.bfloat16

P = 128
SEQ = 256
TILES = 4
BLOCK = TILES * P
SEQS = BLOCK // SEQ
HEADS, HD = 8, 16
TAPS = 5
PROJ, RANKS = 32, (1, 2, 4, 8)
RANK_SUM, RANK_PAD = sum(RANKS), 16
EXPERTS, GROUPS, EF = 16, 4, 64
CHUNKS = EXPERTS * EF // P
ALLCH = CHUNKS + 1
EPS = 1e-5
CLAMP_MAX = float(np.log(1.0 / 0.01))
A_SCALE = HD ** -0.5
C_SCALE = P ** -0.5
MASKED = -9.0e15

SPLIT_COLS = {}
WHOLE_COLS = {}


def _place(table, parts):
    at = 0
    for name, width in parts:
        table[name] = (at, at + width)
        at += width
    return at


N_SPLIT = _place(SPLIT_COLS, [("qk", 2 * P), ("v", P), ("g", P), ("base", P), ("proj", PROJ), ("logit", len(RANKS)),
                              ("down", RANK_PAD), ("cq", P), ("ck", P), ("cv", P), ("gate", EXPERTS),
                              ("w1", ALLCH * P), ("w3", ALLCH * P)])
N_WHOLE = _place(WHOLE_COLS, [("wo", P), ("w2", ALLCH * P), ("cos", BLOCK), ("sin", BLOCK), ("hmask", P), ("hmask8", HEADS),
                              ("ident", P), ("taps", TAPS), ("tapb", 1), ("bp", PROJ), ("bcq", 1), ("bck", 1),
                              ("bcv", P), ("causal", P), ("order", len(RANKS)), ("before", GROUPS * GROUPS), ("temp", 1),
                              ("wp", P), ("sim", len(RANKS)), ("bprep", P), ("ones", P), ("up", P),
                              ("sel_head", P), ("sel_exp", CHUNKS * P),
                              ("zero", TILES * EXPERTS), ("carry", TILES * EXPERTS), ("half", TILES), ("neg_half", TILES), ("quarter", TILES),
                              ("inv_p", TILES), ("eps", TILES)])


class Signal:

    def __init__(self, sem, per):
        self.sem, self.per = sem, per

    def at(self, n, k=None):
        return n * self.per + (self.per if k is None else k)


def started(n):
    return not (isinstance(n, int) and n == 0)


def n_is(n, least):
    return not isinstance(n, int) or n >= least


def build(nc, x_dram, split_dram, whole_dram, out_dram):
    blocks = x_dram.shape[0] // BLOCK
    LEAD = 6
    loops = (blocks - LEAD) // 2
    turns = blocks + 4
    assert blocks % 2 == 0 and loops > 0

    def live(n):
        return not isinstance(n, int) or 0 <= n < blocks

    x_view = x_dram.rearrange("(n t p) d -> n p t d", t=TILES, p=P)
    out_view = out_dram.rearrange("(n t p) d -> n p t d", t=TILES, p=P)

    with ExitStack() as ctx:
        def sb(name, shape, dt=F32):
            return ctx.enter_context(nc.sbuf_tensor(name, shape, dt))

        def sig(name, per=1):
            return Signal(ctx.enter_context(nc.semaphore(name)), per)

        bank = [ctx.enter_context(nc.psum_tensor(f"bank{i}", [P, BLOCK], F32)) for i in range(8)]
        GB, UB, CB, YB = bank[0:4]
        A0, A1 = bank[4:6]
        B0, B1 = bank[6:8]

        w_raw = sb("w_raw", [P, N_SPLIT])
        w_hi = sb("w_hi", [P, N_SPLIT], F32R)
        w_lo = sb("w_lo", [P, N_SPLIT], F32R)
        whole = sb("whole", [P, N_WHOLE])

        def hi(name, a=0, b=None):
            lo_, up_ = SPLIT_COLS[name]
            return w_hi[:, lo_ + a:(up_ if b is None else lo_ + b)]

        def lo(name, a=0, b=None):
            lo_, up_ = SPLIT_COLS[name]
            return w_lo[:, lo_ + a:(up_ if b is None else lo_ + b)]

        def const(name, parts=P):
            a, b = WHOLE_COLS[name]
            return whole[0:parts, a:b]

        ident = const("ident")
        ident_b = sb("ident_b", [P, P], BF16)
        causal_b = sb("causal_b", [P, P], BF16)
        sel_head_b = sb("sel_head_b", [3 * HEADS, P], BF16)
        sel_exp_b = sb("sel_exp_b", [3 * EXPERTS, CHUNKS * P], BF16)
        clamp_t = sb("clamp_t", [P, 1])
        escale = sb("escale", [P, 1])
        sim_sq = sb("sim_sq", [PROJ, 4])
        sim_n2 = sb("sim_n2", [PROJ, 4])
        sim_rn = sb("sim_rn", [PROJ, 4])
        sim_n = sb("sim_n", [PROJ, 4])
        sim_s = sb("sim_s", [PROJ, 4])
        bp_logit = sb("bp_logit", [P, 4])
        bcq_s = sb("bcq_s", [P, 1])

        x_in = sb("x_in", [P, 2, TILES, P])
        xT = [sb(f"x{k}T", [P, BLOCK]) for k in range(4)]
        x3T_hi = [sb(f"x3T_hi{i}", [P, BLOCK], F32R) for i in range(2)]
        x3T_lo = [sb(f"x3T_lo{i}", [P, BLOCK], F32R) for i in range(2)]
        combT = [sb(f"combT{i}", [3 * EXPERTS, BLOCK], BF16) for i in range(2)]
        x3 = [sb(f"x3_{i}", [P, TILES, P]) for i in range(2)]
        rope_c = sb("rope_c", [P, 2, BLOCK])
        rope_s = sb("rope_s", [P, 2, BLOCK])
        qk = sb("qk", [P, TILES, 2 * P])
        v_one = sb("v_one", [P, TILES, P + 1])
        gT = sb("gT", [P, BLOCK])
        kv_m = sb("kv_m", [P, SEQS, P])
        ks_m = sb("ks_m", [P, SEQS, HEADS])
        v_sum = sb("v_sum", [P, SEQS])
        qT = sb("qT", [P, BLOCK])
        vT = sb("vT", [P, SEQS, SEQ + 4])
        conv = sb("conv", [P, SEQS, SEQ])
        den = sb("den", [P, TILES * HEADS])
        rden = sb("rden", [P, TILES, HEADS])
        rden_r = sb("rden_r", [P, TILES, HEADS])
        rden_b = sb("rden_b", [P, TILES, 3, HEADS], BF16)
        rdenT = sb("rdenT", [3 * HEADS, BLOCK], BF16)
        numT = sb("numT", [P, BLOCK])
        attT = sb("attT", [P, BLOCK])
        mixT = sb("mixT", [P, BLOCK])
        oT = sb("oT", [P, BLOCK])
        res = [sb(f"res{k}", [P, TILES, P]) for k in range(4)]
        stats = [sb(f"stats{k}", [P, TILES, 6]) for k in range(4)]
        moment = [sb(f"moment{k}", [P, 8, TILES]) for k in range(4)]
        mean = [sb(f"mean{k}", [P, TILES]) for k in range(4)]
        rstd = [sb(f"rstd{k}", [P, TILES]) for k in range(4)]
        x1, x2, x4 = (sb(name, [P, TILES, P]) for name in ("x1", "x2", "x4"))
        x2_b = sb("x2_b", [P, TILES, P])
        centered = sb("centered", [P, TILES, P])
        proj = sb("proj", [P, TILES, PROJ])
        proj_sq = sb("proj_sq", [P, TILES, PROJ])
        proj_n2 = sb("proj_n2", [P, TILES])
        proj_n2c = sb("proj_n2c", [P, TILES])
        proj_rn = sb("proj_rn", [P, TILES])
        lg_b = sb("lg_b", [P, TILES, 4])
        lg = sb("lg", [P, TILES, 4])
        lg_max = sb("lg_max", [P, TILES])
        lg_s = sb("lg_s", [P, TILES, 4])
        lg_e = sb("lg_e", [P, TILES, 4])
        lg_sum = sb("lg_sum", [P, TILES])
        lw_max = sb("lw_max", [P, TILES])
        cand = sb("cand", [P, TILES, 4])
        cand_max = sb("cand_max", [P, TILES])
        first = sb("first", [P, TILES, 4])
        ret = sb("ret", [P, TILES, 4])
        down_m = sb("down_m", [P, TILES, RANK_PAD])
        downT = sb("downT", [RANK_PAD, BLOCK])
        cqT = sb("cqT", [P, BLOCK])
        ckT = sb("ckT", [P, BLOCK])
        cv = sb("cv", [P, TILES, P])
        neg_max = sb("neg_max", [P, TILES])
        prob = sb("prob", [P, SEQS, 3 * P])
        row_sum = sb("row_sum", [P, TILES])
        row_inv = sb("row_inv", [P, TILES])
        probT = sb("probT", [P, SEQS, 3 * P])
        ez = sb("ez", [P, TILES * EXPERTS])
        ez1 = sb("ez1", [P, TILES * EXPERTS])
        score = sb("score", [P, TILES, EXPERTS])
        pair_hi = sb("pair_hi", [P, TILES * 8])
        pair_sum = sb("pair_sum", [P, TILES * 8])
        cross = sb("cross", [P, TILES * 4])
        inner = sb("inner", [P, TILES * 4])
        gscore = sb("gscore", [P, TILES, GROUPS])
        g_diff = sb("g_diff", [P, TILES, GROUPS, GROUPS])
        g_tie = sb("g_tie", [P, TILES, GROUPS, GROUPS])
        g_beat = sb("g_beat", [P, TILES, GROUPS, GROUPS])
        g_rank = sb("g_rank", [P, TILES, GROUPS])
        penalty = sb("penalty", [P, TILES, GROUPS])
        masked = sb("masked", [P, TILES, EXPERTS])
        top8 = sb("top8", [P, TILES, 8])
        above = sb("above", [P, TILES, EXPERTS])
        n_above = sb("n_above", [P, TILES])
        equal = sb("equal", [P, TILES, EXPERTS])
        count = sb("count", [P, TILES, EXPERTS])
        place = sb("place", [P, TILES, EXPERTS])
        tied = sb("tied", [P, TILES, EXPERTS])
        chosen = sb("chosen", [P, TILES, EXPERTS])
        wsel = sb("wsel", [P, TILES, EXPERTS])
        wsum = sb("wsum", [P, TILES])
        wsum_e = sb("wsum_e", [P, TILES])
        winv = sb("winv", [P, TILES])
        comb = sb("comb", [P, TILES, EXPERTS])
        comb_r = sb("comb_r", [P, TILES, EXPERTS])
        comb_b = sb("comb_b", [P, TILES, 6, EXPERTS], BF16)
        silu = sb("silu", [P, 2, BLOCK])
        gu = sb("gu", [P, 2, BLOCK])
        hid = sb("hid", [P, 2, BLOCK])
        yT = sb("yT", [P, BLOCK])

        w_in, k_in, x_st = sig("w_in"), sig("k_in"), sig("x_st", 16)
        x_ld = [sig(f"x_ld{i}", 16) for i in range(2)]
        setup_v, setup_a, setup_p, setup_g = sig("setup_v"), sig("setup_a"), sig("setup_p"), sig("setup_g")
        p_xT = [sig(f"p_x{k}T") for k in range(4)]
        a_xT = [sig(f"a_x{k}T") for k in range(4)]
        a_x3h, g_x3l = sig("a_x3h"), sig("g_x3l")
        p_qk, p_v, p_g, p_kv = sig("p_qk", 2), sig("p_v"), sig("p_g"), sig("p_kv")
        p_qT, p_vT, p_den, p_num = sig("p_qT"), sig("p_vT"), sig("p_den"), sig("p_num")
        p_rdT, p_rd, p_y = sig("p_rdT"), sig("p_rd"), sig("p_y")
        v_rope, g_qk, a_v, a_g = sig("v_rope", 6), sig("g_qk", 2), sig("a_v"), sig("a_g")
        v_kv, a_qT, a_vT, a_tap, v_conv = sig("v_kv", 3), sig("a_qT"), sig("a_vT"), sig("a_tap"), sig("v_conv", TAPS - 1)
        v_den, v_rden, g_rd, a_num, a_rdT = sig("v_den"), sig("v_rden"), sig("g_rd", 4), sig("a_num", 2), sig("a_rdT")
        v_att, g_mix, v_oT = sig("v_att"), sig("g_mix"), sig("v_oT")
        v_res = [sig(f"v_res{k}", TILES if k == 2 else 1) for k in range(4)]
        v_st = [sig(f"v_st{k}", TILES) for k in range(4)]
        g_ln = [sig(f"g_ln{k}", 10) for k in range(4)]
        v_x = [sig(f"v_x{k + 1}", TILES) for k in range(3)]
        g_cent, g_x4 = sig("g_cent"), sig("g_x4")
        p_small, p_dnT, p_up = sig("p_small"), sig("p_dnT"), sig("p_up")
        B_NORM2, B_LOGITS = 5, 8
        v_b, g_b, a_b, v_down, a_dnT = sig("v_b", 14), sig("g_b"), sig("a_b"), sig("v_down", 4), sig("a_dnT")
        g_x2b = sig("g_x2b")
        p_cq, p_ck, p_cv, p_s, p_pT, p_av = sig("p_cq"), sig("p_ck"), sig("p_cv"), sig("p_s", 2), sig("p_pT", 2), sig("p_av")
        a_cq, a_ck, a_cv, v_max, a_exp, a_pT, v_rinv = (sig("a_cq"), sig("a_ck"), sig("a_cv"), sig("v_max", 4),
                                                        sig("a_exp", 4), sig("a_pT", 2), sig("v_rinv"))
        R_GROUPS, R_MASKED, R_TOP = 7, 13, 17
        p_gate, a_ez, v_r, g_c, p_cT, a_cT = sig("p_gate"), sig("a_ez"), sig("v_r", 29), sig("g_c", 4), sig("p_cT"), sig("a_cT")
        p_G, p_U, p_C, p_w2, p_yT = sig("p_G", ALLCH), sig("p_U", ALLCH), sig("p_C", CHUNKS), sig("p_w2", ALLCH), sig("p_yT")
        a_silu, v_gu, v_hid, a_y = sig("a_silu", ALLCH), sig("v_gu", ALLCH), sig("v_hid", CHUNKS), sig("a_y")

        block = ctx.enter_context(nc.Block())

        @block.sync
        def _(sp):
            nc.sync.dma_start(whole[:], whole_dram).then_inc(k_in.sem, 16)
            nc.sync.dma_start(w_raw[:], split_dram).then_inc(w_in.sem, 16)
            nc.sync.dma_start(x_in[:, 0], x_view[0]).then_inc(x_ld[0].sem, 16)
            nc.sync.dma_start(x_in[:, 1], x_view[1]).then_inc(x_ld[1].sem, 16)

            def load_after(n, half):
                sp.wait_ge(v_res[0].sem, v_res[0].at(n))
                nc.sync.dma_start(x_in[:, half], x_view[n + 2]).then_inc(x_ld[half].sem, 16)

            def store(n):
                sp.wait_ge(g_x4.sem, g_x4.at(n))
                nc.sync.dma_start(out_view[n], x4[:]).then_inc(x_st.sem, 16)

            for n in range(4):
                load_after(n, n % 2)
            with sp.Fori(0, blocks // 2 - 3) as k:
                store(2 * k)
                load_after(2 * k + 4, 0)
                store(2 * k + 1)
                load_after(2 * k + 5, 1)
            for n in range(blocks - 6, blocks):
                store(n)
            sp.wait_ge(x_st.sem, x_st.at(blocks - 1))

        @block.tensor
        def _(pe):
            mm = nc.tensor.matmul

            def mm3(out, wh, wl, mh, ml):
                mm(out, wh, mh, start=True, stop=False)
                mm(out, wh, ml, start=False, stop=False)
                return mm(out, wl, mh, start=False, stop=True)

            def tile(ap, t):
                return ap[:, t * P:(t + 1) * P]

            def transpose_tiles(out, src, eye, parts=P):
                for t in range(TILES):
                    last = nc.tensor.transpose(out[0:parts, t * P:(t + 1) * P], src(t), eye)
                return last

            def raw(name, a=0, b=None):
                first, end = SPLIT_COLS[name]
                return w_raw[:, first + a:(end if b is None else first + b)]

            pe.wait_ge(k_in.sem, 16)
            pe.wait_ge(setup_v.sem, 1)
            mm(A0[0:PROJ, 0:4], const("ones", PROJ)[:, 0:PROJ], sim_sq[:], start=True, stop=True).then_inc(setup_p.sem, 1)
            pe.wait_ge(setup_v.sem, 4)
            mm(A1[:, 0:4], const("wp", PROJ), sim_s[:], start=True, stop=True)
            mm(B0[:, 0:4], const("bprep", PROJ), sim_s[:], start=True, stop=True).then_inc(setup_p.sem, 1)
            pe.wait_ge(setup_v.sem, 12)
            pe.wait_ge(setup_a.sem, 3)

            def a_xT_(n, half, load):
                pe.wait_ge(x_ld[half].sem, x_ld[half].at(load))
                if started(n):
                    pe.wait_ge(v_att.sem, v_att.at(n - 1))
                transpose_tiles(A0, lambda t: x_in[:, half, t], ident).then_inc(p_xT[0].sem, 1)

            def a_qk(n):
                pe.wait_ge(a_xT[0].sem, a_xT[0].at(n))
                if started(n):
                    pe.wait_ge(v_res[0].sem, v_res[0].at(n - 1))
                for h, b in ((0, A1), (1, A0)):
                    for i in range(2):
                        last = mm(b[:, i * 2 * P:(i + 1) * 2 * P], tile(xT[0], 2 * h + i), raw("qk"), start=True, stop=True)
                    last.then_inc(p_qk.sem, 1)

            def a_vg(n):
                pe.wait_ge(v_rope.sem, v_rope.at(n, 3))
                for t in range(TILES):
                    last = mm(tile(A1, t), tile(xT[0], t), raw("v"), start=True, stop=True)
                last.then_inc(p_v.sem, 1)
                pe.wait_ge(v_rope.sem, v_rope.at(n))
                mm(A0[:], raw("g"), xT[0][:], start=True, stop=True).then_inc(p_g.sem, 1)

            def a_kv(n):
                pe.wait_ge(g_qk.sem, g_qk.at(n))
                pe.wait_ge(a_v.sem, a_v.at(n))
                for s in range(SEQS):
                    for i in range(2):
                        mm(A1[:, s * SEQ:s * SEQ + P + 1], qk[:, 2 * s + i, P:2 * P], v_one[:, 2 * s + i, :],
                           start=i == 0, stop=i == 1)
                    for i in range(2):
                        last = mm(A1[:, s * SEQ + P + 1:s * SEQ + P + 2], v_one[:, 2 * s + i, 0:P],
                                  v_one[:, 2 * s + i, P:P + 1], start=i == 0, stop=i == 1)
                last.then_inc(p_kv.sem, 1)

            def a_qvT(n):
                pe.wait_ge(a_g.sem, a_g.at(n))
                transpose_tiles(A0, lambda t: qk[:, t, 0:P], ident).then_inc(p_qT.sem, 1)
                pe.wait_ge(v_kv.sem, v_kv.at(n))
                transpose_tiles(A1, lambda t: v_one[:, t, 0:P], ident).then_inc(p_vT.sem, 1)

            def a_den(n):
                pe.wait_ge(a_qT.sem, a_qT.at(n))
                pe.wait_ge(a_vT.sem, a_vT.at(n))
                for t in range(TILES):
                    last = mm(A1[:, t * HEADS:(t + 1) * HEADS], tile(qT, t), ks_m[:, t // 2, :], start=True, stop=True)
                last.then_inc(p_den.sem, 1)
                for s in range(SEQS):
                    last = mm(A0[:, s * SEQ:(s + 1) * SEQ], kv_m[:, s, :], qT[:, s * SEQ:(s + 1) * SEQ], start=True, stop=True)
                last.then_inc(p_num.sem, 1)

            def a_rdT_(n):
                pe.wait_ge(g_rd.sem, g_rd.at(n))
                transpose_tiles(A1[:].bitcast(BF16), lambda t: rden_b[:, t].rearrange("p a h -> p (a h)"), ident_b[:],
                                parts=3 * HEADS).then_inc(p_rdT.sem, 1)

            def a_rd(n):
                pe.wait_ge(a_num.sem, a_num.at(n))
                pe.wait_ge(a_rdT.sem, a_rdT.at(n))
                mm(A0[:], sel_head_b[:], rdenT[:], start=True, stop=True).then_inc(p_rd.sem, 1)

            def a_out(n):
                pe.wait_ge(v_oT.sem, v_oT.at(n))
                for t in range(TILES):
                    last = mm(tile(A1, t), tile(oT, t), const("wo"), start=True, stop=True)
                last.then_inc(p_y.sem, 1)

            def b_xT(n):
                pe.wait_ge(v_x[0].sem, v_x[0].at(n))
                if n_is(n, 2):
                    pe.wait_ge(a_cT.sem, a_cT.at(n - 2))
                elif started(n):
                    pe.wait_ge(a_pT.sem, a_pT.at(n - 1))
                transpose_tiles(B0, lambda t: x1[:, t], ident).then_inc(p_xT[1].sem, 1)

            def b_small(n):
                pe.wait_ge(a_xT[1].sem, a_xT[1].at(n))
                a, b = SPLIT_COLS["proj"][0], SPLIT_COLS["down"][1]
                w = b - a
                for t in range(TILES):
                    last = mm(B0[:, t * w:(t + 1) * w], tile(xT[1], t), w_raw[:, a:b], start=True, stop=True)
                last.then_inc(p_small.sem, 1)

            def b_dnT(n):
                pe.wait_ge(v_down.sem, v_down.at(n))
                transpose_tiles(B0, lambda t: down_m[:, t, :], ident, parts=RANK_PAD).then_inc(p_dnT.sem, 1)

            def b_up(n):
                pe.wait_ge(a_dnT.sem, a_dnT.at(n))
                if started(n):
                    pe.wait_ge(a_ez.sem, a_ez.at(n - 1))
                for t in range(TILES):
                    mm(tile(B1, t), tile(xT[1], t), raw("base"), start=True, stop=False)
                    last = mm(tile(B1, t), tile(downT, t), const("up", RANK_PAD), start=False, stop=True)
                last.then_inc(p_up.sem, 1)

            def c_xT(n):
                pe.wait_ge(v_x[1].sem, v_x[1].at(n))
                transpose_tiles(B0, lambda t: x2[:, t], ident).then_inc(p_xT[2].sem, 1)

            def c_project(n):
                pe.wait_ge(a_xT[2].sem, a_xT[2].at(n))
                mm(B1[:], raw("cq"), xT[2][:], start=True, stop=True).then_inc(p_cq.sem, 1)
                mm(B0[:], raw("ck"), xT[2][:], start=True, stop=True).then_inc(p_ck.sem, 1)
                pe.wait_ge(a_cq.sem, a_cq.at(n))
                for t in range(TILES):
                    last = mm(tile(B1, t), tile(xT[2], t), raw("cv"), start=True, stop=True)
                last.then_inc(p_cv.sem, 1)

            def c_scores(n):
                pe.wait_ge(a_ck.sem, a_ck.at(n))
                for s, b in ((0, B0), (1, B1)):
                    if s == 1:
                        pe.wait_ge(a_cv.sem, a_cv.at(n))
                    q0, q1 = tile(cqT, 2 * s), tile(cqT, 2 * s + 1)
                    k0, k1 = tile(ckT, 2 * s), tile(ckT, 2 * s + 1)
                    mm(b[:, 0:P], ident_b[:], causal_b[:], start=True, stop=False)
                    mm(b[:, 0:P], q0, k0, start=False, stop=True)
                    mm(b[:, P:2 * P], q1, k0, start=True, stop=True)
                    mm(b[:, 2 * P:3 * P], ident_b[:], causal_b[:], start=True, stop=False)
                    mm(b[:, 2 * P:3 * P], q1, k1, start=False, stop=True).then_inc(p_s.sem, 1)

            def c_pT(n):
                for s, b in ((0, B0), (1, B1)):
                    pe.wait_ge(a_exp.sem, a_exp.at(n, 2 * s + 2))
                    for i in range(3):
                        last = nc.tensor.transpose(b[:, i * P:(i + 1) * P], prob[:, s, i * P:(i + 1) * P], ident)
                    last.then_inc(p_pT.sem, 1)

            def c_av(n):
                pe.wait_ge(a_pT.sem, a_pT.at(n))
                for s in range(SEQS):
                    mm(tile(B1, 2 * s), probT[:, s, 0:P], cv[:, 2 * s], start=True, stop=True)
                    mm(tile(B1, 2 * s + 1), probT[:, s, P:2 * P], cv[:, 2 * s], start=True, stop=False)
                    last = mm(tile(B1, 2 * s + 1), probT[:, s, 2 * P:3 * P], cv[:, 2 * s + 1], start=False, stop=True)
                last.then_inc(p_av.sem, 1)

            def r_xT(n, odd):
                pe.wait_ge(v_x[2].sem, v_x[2].at(n))
                transpose_tiles(B1, lambda t: x3[odd][:, t], ident).then_inc(p_xT[3].sem, 1)

            def r_gate(n):
                pe.wait_ge(a_x3h.sem, a_x3h.at(n))
                for t in range(TILES):
                    last = mm(B1[:, t * EXPERTS:(t + 1) * EXPERTS], tile(xT[3], t), raw("gate"), start=True, stop=True)
                last.then_inc(p_gate.sem, 1)

            def r_cT(n, behind):
                pe.wait_ge(g_c.sem, g_c.at(n))
                if behind:
                    pe.wait_ge(a_pT.sem, a_pT.at(n + 1, 1))
                transpose_tiles(B0[:].bitcast(BF16), lambda t: comb_b[:, t].rearrange("p a e -> p (a e)"), ident_b[:],
                                parts=6 * EXPERTS).then_inc(p_cT.sem, 1)

            def d_hidden(n, odd, c):
                xh, xl = x3T_hi[odd], x3T_lo[odd]
                if c == 0:
                    pe.wait_ge(a_cT.sem, a_cT.at(n))
                    pe.wait_ge(g_x3l.sem, g_x3l.at(n))
                if c > 0 or started(n):
                    pe.wait_ge(a_silu.sem, a_silu.at(n, c))
                w = c * P, (c + 1) * P
                mm3(GB[:], hi("w1", *w), lo("w1", *w), xh[:], xl[:]).then_inc(p_G.sem, 1)
                if c > 0 or started(n):
                    pe.wait_ge(v_gu.sem, v_gu.at(n, c))
                mm3(UB[:], hi("w3", *w), lo("w3", *w), xh[:], xl[:]).then_inc(p_U.sem, 1)
                if c < CHUNKS:
                    if c > 0 or started(n):
                        pe.wait_ge(v_hid.sem, v_hid.at(n, c))
                    mm(CB[:], sel_exp_b[:, c * P:(c + 1) * P], combT[odd][:], start=True, stop=True).then_inc(p_C.sem, 1)

            def d_down(n, c):
                if c < CHUNKS:
                    pe.wait_ge(v_hid.sem, v_hid.at(n, c + 1))
                else:
                    pe.wait_ge(v_gu.sem, v_gu.at(n))
                if c == 0 and started(n):
                    pe.wait_ge(v_res[3].sem, v_res[3].at(n - 1))
                a = WHOLE_COLS["w2"][0] + c * P
                mm(YB[:], whole[:, a:a + P], hid[:, c % 2], start=c == 0, stop=c == CHUNKS).then_inc(p_w2.sem, 1)

            def d_yT(n):
                pe.wait_ge(a_y.sem, a_y.at(n))
                transpose_tiles(YB, lambda t: tile(yT, t), ident).then_inc(p_yT.sem, 1)

            def turn(i, odd, load=None):
                a, bc, r, d, e = live(i), live(i - 1), live(i - 2), live(i - 3), live(i - 4)
                if d: d_hidden(i - 3, 1 - odd, 0)
                if e: d_yT(i - 4)
                if a: a_xT_(i, odd, load)
                if bc: b_xT(i - 1)
                if r: r_xT(i - 2, odd)
                if d: d_hidden(i - 3, 1 - odd, 1)
                if bc: b_small(i - 1)
                if r: r_gate(i - 2)
                if d: d_down(i - 3, 0)
                if a: a_qk(i)
                if d: d_hidden(i - 3, 1 - odd, 2)
                if d: d_down(i - 3, 1)
                if a: a_vg(i)
                if bc: b_dnT(i - 1)
                if d: d_hidden(i - 3, 1 - odd, 3)
                if bc: b_up(i - 1)
                if d: d_down(i - 3, 2)
                if a: a_kv(i)
                if d: d_hidden(i - 3, 1 - odd, 4)
                if a: a_qvT(i)
                if d: d_down(i - 3, 3)
                if bc: c_xT(i - 1)
                if a: a_den(i)
                if d: d_hidden(i - 3, 1 - odd, 5)
                if bc: c_project(i - 1)
                if d: d_down(i - 3, 4)
                if a: a_rdT_(i)
                if d: d_hidden(i - 3, 1 - odd, 6)
                if bc: c_scores(i - 1)
                if a: a_rd(i)
                if d: d_down(i - 3, 5)
                if d: d_hidden(i - 3, 1 - odd, 7)
                if bc: c_pT(i - 1)
                if d: d_down(i - 3, 6)
                if a: a_out(i)
                if d: d_hidden(i - 3, 1 - odd, 8)
                if r: r_cT(i - 2, bc)
                if d: d_down(i - 3, 7)
                if bc: c_av(i - 1)
                if d: d_down(i - 3, 8)

            for i in range(LEAD):
                turn(i, i % 2, i // 2)
            with pe.Fori(0, loops) as k:
                turn(2 * k + LEAD, 0, k + LEAD // 2)
                turn(2 * k + LEAD + 1, 1, k + LEAD // 2)
            for i in range(blocks, turns):
                turn(i, i % 2)

        @block.scalar
        def _(act):
            fn = nc.scalar.activation
            act.wait_ge(k_in.sem, 16)
            act.wait_ge(setup_v.sem, 2)
            fn(escale[:], clamp_t[:], ACT.Exp).then_inc(setup_a.sem, 1)
            act.wait_ge(setup_v.sem, 5)
            fn(w_hi[:], w_raw[:], ACT.Copy).then_inc(setup_a.sem, 1)
            fn(bcq_s[:], const("bcq"), ACT.Copy, scale=C_SCALE).then_inc(setup_a.sem, 1)
            act.wait_ge(setup_a.sem, 3)
            act.wait_ge(setup_v.sem, 12)

            def copy_xT(n, k, b):
                act.wait_ge(p_xT[k].sem, p_xT[k].at(n))
                fn(xT[k][:], b[:], ACT.Copy).then_inc(a_xT[k].sem, 1)

            def a_evac(n):
                act.wait_ge(p_v.sem, p_v.at(n))
                fn(v_one[:, :, 0:P], A1[:].rearrange("p (t d) -> p t d", t=TILES), ACT.Copy).then_inc(a_v.sem, 1)
                act.wait_ge(p_g.sem, p_g.at(n))
                fn(gT[:], A0[:], ACT.Copy).then_inc(a_g.sem, 1)

            def a_qv(n):
                act.wait_ge(p_qT.sem, p_qT.at(n))
                fn(qT[:], A0[:], ACT.Copy).then_inc(a_qT.sem, 1)
                act.wait_ge(p_vT.sem, p_vT.at(n))
                fn(vT[:, :, 2:2 + SEQ], A1[:].rearrange("p (s l) -> p s l", s=SEQS), ACT.Copy).then_inc(a_vT.sem, 1)
                act.wait_ge(a_vT.sem, a_vT.at(n))
                fn(conv[:], vT[:, :, 0:SEQ], ACT.Identity, scale=const("taps")[:, 0:1],
                   bias=const("tapb")).then_inc(a_tap.sem, 1)

            def a_numv(n):
                act.wait_ge(p_num.sem, p_num.at(n))
                act.wait_ge(v_kv.sem, v_kv.at(n))
                for s in range(SEQS):
                    fn(numT[:, s * SEQ:(s + 1) * SEQ], A0[:, s * SEQ:(s + 1) * SEQ], ACT.Identity,
                       bias=v_sum[:, s:s + 1]).then_inc(a_num.sem, 1)

            def a_rdT_(n):
                act.wait_ge(p_rdT.sem, p_rdT.at(n))
                fn(rdenT[:], A1[:].bitcast(BF16)[0:3 * HEADS, 0:BLOCK], ACT.Copy).then_inc(a_rdT.sem, 1)

            def b_exp(n):
                act.wait_ge(v_b.sem, v_b.at(n, B_LOGITS))
                fn(lg_e[:], lg_s[:], ACT.Exp).then_inc(a_b.sem, 1)

            def b_dnT(n):
                act.wait_ge(p_dnT.sem, p_dnT.at(n))
                fn(downT[:], B0[0:RANK_PAD, :], ACT.Copy).then_inc(a_dnT.sem, 1)

            def c_qkv(n):
                act.wait_ge(p_cq.sem, p_cq.at(n))
                fn(cqT[:], B1[:], ACT.Identity, scale=C_SCALE, bias=bcq_s[:]).then_inc(a_cq.sem, 1)
                act.wait_ge(p_ck.sem, p_ck.at(n))
                fn(ckT[:], B0[:], ACT.Identity, bias=const("bck")).then_inc(a_ck.sem, 1)
                act.wait_ge(p_cv.sem, p_cv.at(n))
                fn(cv[:].rearrange("p t d -> p (t d)"), B1[:], ACT.Copy).then_inc(a_cv.sem, 1)

            def c_exp(n):
                for s, b in ((0, B0), (1, B1)):
                    act.wait_ge(v_max.sem, v_max.at(n, 2 * s + 2))
                    for i, (a, w) in enumerate(((0, P), (P, 2 * P))):
                        t = 2 * s + i
                        fn(prob[:, s, a:a + w], b[:, a:a + w], ACT.Exp, bias=neg_max[:, t:t + 1],
                           accum_out=row_sum[:, t:t + 1]).then_inc(a_exp.sem, 1)

            def c_pT(n):
                for s, b in ((0, B0), (1, B1)):
                    act.wait_ge(p_pT.sem, p_pT.at(n, s + 1))
                    fn(probT[:, s, :], b[:, 0:3 * P], ACT.Copy).then_inc(a_pT.sem, 1)

            def r_hi(n, odd):
                act.wait_ge(p_xT[3].sem, p_xT[3].at(n))
                fn(xT[3][:], B1[:], ACT.Copy).then_inc(a_xT[3].sem, 1)
                fn(x3T_hi[odd][:], B1[:], ACT.Copy).then_inc(a_x3h.sem, 1)

            def r_exp(n):
                act.wait_ge(p_gate.sem, p_gate.at(n))
                fn(ez[:], B1[:, 0:TILES * EXPERTS], ACT.Exp, scale=-1.0).then_inc(a_ez.sem, 1)

            def r_cT(n, odd):
                act.wait_ge(p_cT.sem, p_cT.at(n))
                fn(combT[odd][:], B0[:].bitcast(BF16)[0:3 * EXPERTS, 0:BLOCK], ACT.Copy).then_inc(a_cT.sem, 1)

            def d_silu(n, c):
                act.wait_ge(p_G.sem, p_G.at(n, c + 1))
                if c > 1 or started(n):
                    act.wait_ge(v_gu.sem, v_gu.at(n, max(c - 1, 0)))
                fn(silu[:, c % 2], GB[:], ACT.Silu).then_inc(a_silu.sem, 1)

            def d_y(n):
                act.wait_ge(p_w2.sem, p_w2.at(n))
                fn(yT[:], YB[:], ACT.Copy).then_inc(a_y.sem, 1)

            def turn(i, odd):
                a, bc, r, d, e = live(i), live(i - 1), live(i - 2), live(i - 3), live(i - 4)
                if d: d_silu(i - 3, 0)
                if a: copy_xT(i, 0, A0)
                if bc: copy_xT(i - 1, 1, B0)
                if r: r_hi(i - 2, odd)
                if d: d_silu(i - 3, 1)
                if r: r_exp(i - 2)
                if bc: b_exp(i - 1)
                if d: d_silu(i - 3, 2)
                if a: a_evac(i)
                if bc: b_dnT(i - 1)
                if d: d_silu(i - 3, 3)
                if d: d_silu(i - 3, 4)
                if a: a_qv(i)
                if bc: copy_xT(i - 1, 2, B0)
                if a: a_numv(i)
                if d: d_silu(i - 3, 5)
                if bc: c_qkv(i - 1)
                if a: a_rdT_(i)
                if d: d_silu(i - 3, 6)
                if bc: c_exp(i - 1)
                if d: d_silu(i - 3, 7)
                if bc: c_pT(i - 1)
                if d: d_silu(i - 3, 8)
                if r: r_cT(i - 2, odd)
                if d: d_y(i - 3)

            for i in range(LEAD):
                turn(i, i % 2)
            with act.Fori(0, loops) as k:
                turn(2 * k + LEAD, 0)
                turn(2 * k + LEAD + 1, 1)
            for i in range(blocks, turns):
                turn(i, i % 2)

        @block.vector
        def _(dve):
            tt, ts, stt, red = (nc.vector.tensor_tensor, nc.vector.tensor_scalar, nc.vector.scalar_tensor_tensor,
                                nc.vector.tensor_reduce)
            dve.wait_ge(k_in.sem, 16)
            sim = const("sim", PROJ)
            tt(sim_sq[:], sim, sim, ALU.mult).then_inc(setup_v.sem, 1)
            ts(clamp_t[:], const("temp"), CLAMP_MAX, None, ALU.min).then_inc(setup_v.sem, 1)
            dve.wait_ge(setup_p.sem, 1)
            ts(sim_n2[:], A0[0:PROJ, 0:4], 1e-24, None, ALU.max).then_inc(setup_v.sem, 1)
            dve.wait_ge(setup_g.sem, 3)
            dve.wait_ge(setup_a.sem, 1)
            stt(sim_s[:], sim, escale[0:PROJ, 0:1], sim_rn[:], ALU.mult, ALU.mult).then_inc(setup_v.sem, 1)
            dve.wait_ge(setup_p.sem, 2)
            dve.wait_ge(w_in.sem, 16)
            a, b = SPLIT_COLS["logit"]
            nc.vector.tensor_copy(w_raw[:, a:b], A1[:, 0:4]).then_inc(setup_v.sem, 1)
            nc.vector.tensor_copy(bp_logit[:], B0[:, 0:4]).then_inc(setup_v.sem, 1)
            nc.vector.tensor_copy(ident_b[:], ident).then_inc(setup_v.sem, 1)
            nc.vector.tensor_copy(causal_b[:], const("causal")).then_inc(setup_v.sem, 1)
            nc.vector.tensor_copy(sel_head_b[:], const("sel_head", 3 * HEADS)).then_inc(setup_v.sem, 1)
            nc.vector.tensor_copy(sel_exp_b[:], const("sel_exp", 3 * EXPERTS)).then_inc(setup_v.sem, 1)
            dve.wait_ge(setup_a.sem, 2)
            dve.wait_ge(setup_v.sem, 5)
            tt(w_lo[:], w_raw[:], w_hi[:].bitcast(F32), ALU.subtract).then_inc(setup_v.sem, 1)
            dve.wait_ge(setup_g.sem, 3 + 3)
            nc.vector.memset(down_m[:], 0.0).then_inc(setup_v.sem, 1)
            dve.wait_ge(setup_v.sem, 12)

            def heads(ap):
                return ap.rearrange("p (h d) -> p h d", d=HD)

            def tiles(ap):
                return ap.rearrange("p (t d) -> p t d", t=TILES)

            def per_tile(ap, w=4):
                return ap.unsqueeze(2).broadcast_to([P, TILES, w])

            def all_tiles(ap, w=4):
                return ap.unsqueeze(1).broadcast_to([P, TILES, w])

            def a_rope(n):
                half = HD // 2
                for h, b in ((0, A1), (1, A0)):
                    dve.wait_ge(p_qk.sem, p_qk.at(n, h + 1))
                    src, sin, out = heads(b[:]), heads(const("sin")), heads(rope_s[:, h])
                    tt(rope_c[:, h], b[:], const("cos"), ALU.mult).then_inc(v_rope.sem, 1)
                    tt(out[:, :, 0:half], src[:, :, half:HD], sin[:, :, 0:half], ALU.mult).then_inc(v_rope.sem, 1)
                    tt(out[:, :, half:HD], src[:, :, 0:half], sin[:, :, half:HD], ALU.mult).then_inc(v_rope.sem, 1)

            def a_kv(n):
                dve.wait_ge(p_kv.sem, p_kv.at(n))
                kv = A1[:].rearrange("p (s c) -> p s c", s=SEQS)
                tt(kv_m[:], kv[:, :, 0:P], const("hmask").unsqueeze(1).broadcast_to([P, SEQS, P]), ALU.mult).then_inc(v_kv.sem, 1)
                tt(ks_m[:], kv[:, :, P:P + 1].broadcast_to([P, SEQS, HEADS]),
                   const("hmask8").unsqueeze(1).broadcast_to([P, SEQS, HEADS]), ALU.mult).then_inc(v_kv.sem, 1)
                nc.vector.tensor_copy(v_sum[:].unsqueeze(2), kv[:, :, P + 1:P + 2]).then_inc(v_kv.sem, 1)

            def a_den(n):
                dve.wait_ge(p_den.sem, p_den.at(n))
                ts(den[:], A1[:, 0:TILES * HEADS], float(SEQ), None, ALU.add).then_inc(v_den.sem, 1)
                dve.wait_ge(v_den.sem, v_den.at(n))
                nc.vector.reciprocal(rden[:].rearrange("p t h -> p (t h)"), den[:]).then_inc(v_rden.sem, 1)

            def a_conv(n):
                dve.wait_ge(a_tap.sem, a_tap.at(n))
                taps = const("taps")
                for j in range(1, TAPS):
                    if j > 1:
                        dve.wait_ge(v_conv.sem, v_conv.at(n, j - 1))
                    stt(conv[:], vT[:, :, j:j + SEQ], taps[:, j:j + 1], conv[:], ALU.mult, ALU.add).then_inc(v_conv.sem, 1)

            def a_att(n):
                dve.wait_ge(p_rd.sem, p_rd.at(n))
                dve.wait_ge(a_num.sem, a_num.at(n))
                tt(attT[:], numT[:], A0[:], ALU.mult).then_inc(v_att.sem, 1)

            def a_gate(n):
                dve.wait_ge(g_mix.sem, g_mix.at(n))
                dve.wait_ge(a_g.sem, a_g.at(n))
                tt(oT[:], mixT[:], gT[:], ALU.mult).then_inc(v_oT.sem, 1)

            def norm_stats(k, n):
                dve.wait_ge(v_res[k].sem, v_res[k].at(n))
                for t in range(TILES):
                    nc.vector.bn_stats(stats[k][:, t, :], res[k][:, t, :]).then_inc(v_st[k].sem, 1)

            def norm_apply(k, n, out):
                dve.wait_ge(g_ln[k].sem, g_ln[k].at(n))
                for t in range(TILES):
                    ts(out[:, t, :], res[k][:, t, :], mean[k][:, t:t + 1], rstd[k][:, t:t + 1],
                       ALU.subtract, ALU.mult).then_inc(v_x[k].sem, 1)

            def a_res(n, half):
                dve.wait_ge(p_y.sem, p_y.at(n))
                tt(res[0][:], x_in[:, half], tiles(A1[:]), ALU.add).then_inc(v_res[0].sem, 1)
                norm_stats(0, n)

            w_small = SPLIT_COLS["down"][1] - SPLIT_COLS["proj"][0]
            small = B0[:, 0:TILES * w_small].rearrange("p (t c) -> p t c", t=TILES)

            def short_steps(n, signal, start):
                done = [start]

                def link(ins, wait=True):
                    ins.then_inc(signal.sem, 1)
                    done[0] += 1
                    if wait:
                        dve.wait_ge(signal.sem, signal.at(n, done[0]))
                return link, done

            def b_norm(n):
                dve.wait_ge(p_small.sem, p_small.at(n))
                link, done = short_steps(n, v_b, 0)
                link(tt(lg_b[:], small[:, :, PROJ:PROJ + 4], all_tiles(bp_logit[:], 4), ALU.add), wait=False)
                link(tt(proj[:], small[:, :, 0:PROJ], all_tiles(const("bp"), PROJ), ALU.add))
                link(tt(proj_sq[:], proj[:], proj[:], ALU.mult))
                link(red(proj_n2[:], proj_sq[:], AX.X, ALU.add))
                link(ts(proj_n2c[:], proj_n2[:], 1e-24, None, ALU.max), wait=False)
                assert done[0] == B_NORM2

            def routes(b, r):
                bb, rr = (lambda k: dve.wait_ge(v_b.sem, v_b.at(b, k))), (lambda k: dve.wait_ge(v_r.sem, v_r.at(r, k)))
                flat = score[:].rearrange("p t e -> p (t e)")
                two = score[:].rearrange("p t (a b) -> p (t a) b", b=2)
                hh = pair_hi[:].rearrange("p (a b) -> p a b", b=2)
                ss = pair_sum[:].rearrange("p (a b) -> p a b", b=2)
                if live(r):
                    dve.wait_ge(a_ez.sem, a_ez.at(r))
                    ts(ez1[:], ez[:], 1.0, None, ALU.add).then_inc(v_r.sem, 1)
                if live(b):
                    dve.wait_ge(g_b.sem, g_b.at(b))
                    tt(lg[:], lg_b[:], per_tile(proj_rn[:]), ALU.mult).then_inc(v_b.sem, 1)
                if live(r):
                    rr(1)
                    nc.vector.reciprocal(flat, ez1[:]).then_inc(v_r.sem, 1)
                if live(b):
                    bb(6)
                    red(lg_max[:], lg[:], AX.X, ALU.max).then_inc(v_b.sem, 1)
                if live(r):
                    rr(2)
                    tt(pair_sum[:], two[:, :, 0], two[:, :, 1], ALU.add).then_inc(v_r.sem, 1)
                    tt(pair_hi[:], two[:, :, 0], two[:, :, 1], ALU.max).then_inc(v_r.sem, 1)
                if live(b):
                    bb(7)
                    tt(lg_s[:], lg[:], per_tile(lg_max[:]), ALU.subtract).then_inc(v_b.sem, 1)
                if live(r):
                    rr(3)
                    tt(inner[:], ss[:, :, 0], ss[:, :, 1], ALU.max).then_inc(v_r.sem, 1)
                    rr(4)
                    tt(cross[:], hh[:, :, 0], hh[:, :, 1], ALU.add).then_inc(v_r.sem, 1)
                if live(b):
                    bb(8)
                    stt(cand[:], lg_s[:], 0.0, all_tiles(const("order")), ALU.is_equal, ALU.mult).then_inc(v_b.sem, 1)
                if live(r):
                    rr(6)
                    tt(gscore[:].rearrange("p t g -> p (t g)"), cross[:], inner[:], ALU.max).then_inc(v_r.sem, 1)
                if live(b):
                    bb(9)
                    red(cand_max[:], cand[:], AX.X, ALU.max).then_inc(v_b.sem, 1)
                if live(r):
                    masked_scores(r, rr, 0)
                if live(b):
                    dve.wait_ge(a_b.sem, a_b.at(b))
                    red(lg_sum[:], lg_e[:], AX.X, ALU.add).then_inc(v_b.sem, 1)
                if live(r):
                    masked_scores(r, rr, 1)
                if live(b):
                    bb(10)
                    tt(first[:], cand[:], per_tile(cand_max[:]), ALU.is_equal).then_inc(v_b.sem, 1)
                    bb(11)
                    nc.vector.reciprocal(lw_max[:], lg_sum[:]).then_inc(v_b.sem, 1)
                if live(r):
                    masked_scores(r, rr, 2)
                if live(b):
                    bb(13)
                    tt(ret[:], first[:], per_tile(lw_max[:]), ALU.mult).then_inc(v_b.sem, 1)
                if live(r):
                    masked_scores(r, rr, 3)
                if live(b):
                    bb(14)
                    at = 0
                    for e, k in enumerate(RANKS):
                        tt(down_m[:, :, at:at + k], small[:, :, PROJ + 4 + at:PROJ + 4 + at + k],
                           ret[:, :, e:e + 1].broadcast_to([P, TILES, k]), ALU.mult).then_inc(v_down.sem, 1)
                        at += k

            def masked_scores(r, rr, part):
                spread = [P, TILES, GROUPS, GROUPS]
                groups = lambda ap: ap.rearrange("p t i j -> p t (i j)")
                if part == 0:
                    rr(7)
                    tt(g_diff[:], gscore[:].unsqueeze(2).broadcast_to(spread), gscore[:].unsqueeze(3).broadcast_to(spread),
                       ALU.subtract).then_inc(v_r.sem, 1)
                if part == 1:
                    rr(8)
                    stt(groups(g_tie[:]), groups(g_diff[:]), 0.0, all_tiles(const("before"), GROUPS * GROUPS),
                        ALU.is_equal, ALU.mult).then_inc(v_r.sem, 1)
                    rr(9)
                    stt(g_beat[:], g_diff[:], 0.0, g_tie[:], ALU.is_gt, ALU.add).then_inc(v_r.sem, 1)
                if part == 2:
                    rr(10)
                    red(g_rank[:], g_beat[:], AX.X, ALU.add).then_inc(v_r.sem, 1)
                if part == 3:
                    rr(11)
                    ts(penalty[:], g_rank[:], 1.5, -3.0, ALU.is_gt, ALU.mult).then_inc(v_r.sem, 1)
                    rr(12)
                    by_group = lambda ap: ap.rearrange("p t (g j) -> p (t g) j", g=GROUPS)
                    tt(by_group(masked[:]), by_group(score[:]),
                       penalty[:].rearrange("p t g -> p (t g)").unsqueeze(2).broadcast_to([P, TILES * GROUPS, EXPERTS // GROUPS]),
                       ALU.add).then_inc(v_r.sem, 1)

            def b_res(n):
                dve.wait_ge(p_up.sem, p_up.at(n))
                tt(res[1][:], x1[:], tiles(B1[:]), ALU.add).then_inc(v_res[1].sem, 1)
                norm_stats(1, n)

            def c_max(n):
                for s, b in ((0, B0), (1, B1)):
                    dve.wait_ge(p_s.sem, p_s.at(n, s + 1))
                    for i, (a, w) in enumerate(((0, P), (P, 2 * P))):
                        red(neg_max[:, 2 * s + i:2 * s + i + 1], b[:, a:a + w], AX.X, ALU.max, negate=True).then_inc(v_max.sem, 1)

            def c_res(n):
                dve.wait_ge(a_exp.sem, a_exp.at(n))
                nc.vector.reciprocal(row_inv[:], row_sum[:]).then_inc(v_rinv.sem, 1)
                dve.wait_ge(v_rinv.sem, v_rinv.at(n))
                dve.wait_ge(p_av.sem, p_av.at(n))
                dve.wait_ge(g_x2b.sem, g_x2b.at(n))
                for t in range(TILES):
                    stt(res[2][:, t, :], B1[:, t * P:(t + 1) * P], row_inv[:, t:t + 1], x2_b[:, t, :],
                        ALU.mult, ALU.add).then_inc(v_res[2].sem, 1)
                norm_stats(2, n)

            def r_combine(n):
                rr = lambda k: dve.wait_ge(v_r.sem, v_r.at(n, k))
                rr(R_MASKED)
                nc.vector.memset(n_above[:], 0.0)
                for t in range(TILES):
                    nc.vector.max(top8[:, t, :], masked[:, t, :]).then_inc(v_r.sem, 1)
                rr(R_TOP)
                fourth = top8[:, :, 3:4].broadcast_to([P, TILES, EXPERTS])
                flat = lambda ap: ap.rearrange("p t e -> p (t e)")
                tt(above[:], masked[:], fourth, ALU.is_gt).then_inc(v_r.sem, 1)
                tt(equal[:], masked[:], fourth, ALU.is_equal).then_inc(v_r.sem, 1)
                rr(R_TOP + 1)
                red(n_above[:], above[:], AX.X, ALU.add).then_inc(v_r.sem, 1)
                rr(R_TOP + 2)
                nc.vector.tensor_tensor_scan(flat(count[:]), const("carry"), flat(equal[:]), 0.0,
                                             ALU.mult, ALU.add).then_inc(v_r.sem, 1)
                rr(R_TOP + 4)
                tt(place[:], count[:], per_tile(n_above[:], EXPERTS), ALU.add).then_inc(v_r.sem, 1)
                rr(R_TOP + 5)
                stt(tied[:], place[:], 4.5, equal[:], ALU.is_lt, ALU.mult).then_inc(v_r.sem, 1)
                rr(R_TOP + 6)
                tt(chosen[:], tied[:], above[:], ALU.add).then_inc(v_r.sem, 1)
                rr(R_TOP + 7)
                tt(wsel[:], chosen[:], score[:], ALU.mult).then_inc(v_r.sem, 1)
                rr(R_TOP + 8)
                red(wsum[:], wsel[:], AX.X, ALU.add).then_inc(v_r.sem, 1)
                rr(R_TOP + 9)
                ts(wsum_e[:], wsum[:], 1e-6, None, ALU.add).then_inc(v_r.sem, 1)
                rr(R_TOP + 10)
                nc.vector.reciprocal(winv[:], wsum_e[:]).then_inc(v_r.sem, 1)
                rr(R_TOP + 11)
                tt(comb[:], wsel[:], per_tile(winv[:], EXPERTS), ALU.mult).then_inc(v_r.sem, 1)

            def d_gu(n, c):
                dve.wait_ge(a_silu.sem, a_silu.at(n, c + 1))
                dve.wait_ge(p_U.sem, p_U.at(n, c + 1))
                if c < CHUNKS:
                    tt(gu[:, c % 2], silu[:, c % 2], UB[:], ALU.mult).then_inc(v_gu.sem, 1)
                else:
                    dve.wait_ge(p_w2.sem, p_w2.at(n, c - 1))
                    tt(hid[:, c % 2], silu[:, c % 2], UB[:], ALU.mult).then_inc(v_gu.sem, 1)

            def d_hid(n, c):
                dve.wait_ge(v_gu.sem, v_gu.at(n, c + 1))
                dve.wait_ge(p_C.sem, p_C.at(n, c + 1))
                if c > 1 or started(n):
                    dve.wait_ge(p_w2.sem, p_w2.at(n, max(c - 1, 0)))
                tt(hid[:, c % 2], gu[:, c % 2], CB[:], ALU.mult).then_inc(v_hid.sem, 1)

            def d_res(n, odd):
                if started(n):
                    dve.wait_ge(g_cent.sem, g_cent.at(n - 1))
                dve.wait_ge(p_yT.sem, p_yT.at(n))
                tt(res[3][:], x3[odd][:], tiles(YB[:]), ALU.add).then_inc(v_res[3].sem, 1)
                norm_stats(3, n)

            def turn(i, odd):
                a, bc, r, d, e = live(i), live(i - 1), live(i - 2), live(i - 3), live(i - 4)
                if d: d_gu(i - 3, 0)
                if e: d_res(i - 4, odd)
                if d: d_hid(i - 3, 0)
                if r: norm_apply(2, i - 2, x3[odd])
                if d: d_gu(i - 3, 1)
                if bc: b_norm(i - 1)
                if d: d_hid(i - 3, 1)
                if a: a_rope(i)
                routes(i - 1, i - 2)
                if d: d_gu(i - 3, 2)
                if d: d_hid(i - 3, 2)
                if d: d_gu(i - 3, 3)
                if bc: b_res(i - 1)
                if d: d_hid(i - 3, 3)
                if a: a_kv(i)
                if d: d_gu(i - 3, 4)
                if bc: norm_apply(1, i - 1, x2)
                if d: d_hid(i - 3, 4)
                if a: a_conv(i)
                if a: a_den(i)
                if d: d_gu(i - 3, 5)
                if r: r_combine(i - 2)
                if d: d_hid(i - 3, 5)
                if d: d_gu(i - 3, 6)
                if bc: c_max(i - 1)
                if d: d_hid(i - 3, 6)
                if a: a_att(i)
                if d: d_gu(i - 3, 7)
                if a: a_gate(i)
                if d: d_hid(i - 3, 7)
                if a: a_res(i, odd)
                if d: d_gu(i - 3, 8)
                if bc: c_res(i - 1)
                if a: norm_apply(0, i, x1)

            for i in range(LEAD):
                turn(i, i % 2)
            with dve.Fori(0, loops) as k:
                turn(2 * k + LEAD, 0)
                turn(2 * k + LEAD + 1, 1)
            for i in range(blocks, turns):
                turn(i, i % 2)

        @block.gpsimd
        def _(pool):
            tt = nc.gpsimd.tensor_tensor
            pool.wait_ge(k_in.sem, 16)
            nc.gpsimd.memset(comb_b[:], 0.0).then_inc(setup_g.sem, 1)
            nc.gpsimd.memset(v_one[:, :, P:P + 1], 1.0).then_inc(setup_g.sem, 1)
            pool.wait_ge(setup_v.sem, 3)
            tt(sim_rn[:], sim_n2[:], const("neg_half", PROJ), ALU.pow).then_inc(setup_g.sem, 1)
            nc.gpsimd.memset(vT[:, :, 0:2], 0.0).then_inc(setup_g.sem, 1)
            nc.gpsimd.memset(vT[:, :, SEQ + 2:SEQ + 4], 0.0).then_inc(setup_g.sem, 1)
            nc.gpsimd.memset(conv[:], 0.0).then_inc(setup_g.sem, 1)

            def a_rope(n):
                for h in range(2):
                    pool.wait_ge(v_rope.sem, v_rope.at(n, 3 * h + 3))
                    tt(qk[:, 2 * h:2 * h + 2, :].rearrange("p t d -> p (t d)"), rope_c[:, h], rope_s[:, h],
                       ALU.add).then_inc(g_qk.sem, 1)

            def split3(n, src, rest, parts, sem, w):
                zeros = const("zero")[:, 0:TILES * w].rearrange("p (t c) -> p t c", t=TILES)
                tt(parts[:, :, 0, :], src[:], zeros, ALU.add).then_inc(sem.sem, 1)
                pool.wait_ge(sem.sem, sem.at(n, 1))
                tt(rest[:], src[:], parts[:, :, 0, :], ALU.subtract).then_inc(sem.sem, 1)
                pool.wait_ge(sem.sem, sem.at(n, 2))
                tt(parts[:, :, 1, :], rest[:], zeros, ALU.add).then_inc(sem.sem, 1)
                pool.wait_ge(sem.sem, sem.at(n, 3))
                tt(parts[:, :, 2, :], rest[:], parts[:, :, 1, :], ALU.subtract).then_inc(sem.sem, 1)

            def a_rd(n):
                pool.wait_ge(v_rden.sem, v_rden.at(n))
                split3(n, rden, rden_r, rden_b[:], g_rd, HEADS)

            def a_mix(n):
                pool.wait_ge(v_att.sem, v_att.at(n))
                pool.wait_ge(v_conv.sem, v_conv.at(n))
                tt(mixT[:], attT[:], conv[:].rearrange("p s l -> p (s l)"), ALU.add).then_inc(g_mix.sem, 1)

            def ln_of(k, n):
                pool.wait_ge(v_st[k].sem, v_st[k].at(n))
                count, m, st = [0], moment[k], stats[k]

                def put(out, in0, in1, op, chained=True):
                    tt(out, in0, in1, op).then_inc(g_ln[k].sem, 1)
                    count[0] += 1
                    if chained:
                        pool.wait_ge(g_ln[k].sem, g_ln[k].at(n, count[0]))

                put(m[:, 0], st[:, :, 1], st[:, :, 4], ALU.add, False)
                put(m[:, 1], st[:, :, 1], st[:, :, 4], ALU.subtract, False)
                put(m[:, 2], st[:, :, 2], st[:, :, 5], ALU.add)
                put(mean[k][:], m[:, 0], const("half"), ALU.mult, False)
                put(m[:, 3], m[:, 1], m[:, 1], ALU.mult, False)
                put(m[:, 4], m[:, 2], const("inv_p"), ALU.mult)
                put(m[:, 5], m[:, 3], const("quarter"), ALU.mult, False)
                put(m[:, 6], m[:, 4], const("eps"), ALU.add)
                put(m[:, 7], m[:, 5], m[:, 6], ALU.add)
                put(rstd[k][:], m[:, 7], const("neg_half"), ALU.pow, False)

            def b_norm(n):
                pool.wait_ge(v_b.sem, v_b.at(n, B_NORM2))
                tt(proj_rn[:], proj_n2c[:], const("neg_half"), ALU.pow).then_inc(g_b.sem, 1)

            def r_split(n):
                pool.wait_ge(v_r.sem, v_r.at(n))
                split3(n, comb, comb_r, comb_b[:, :, 0:3], g_c, EXPERTS)

            def x2_bias(n):
                pool.wait_ge(v_x[1].sem, v_x[1].at(n))
                tt(x2_b[:], x2[:], const("bcv").unsqueeze(1).broadcast_to([P, TILES, P]), ALU.add).then_inc(g_x2b.sem, 1)

            def x3_lo(n, odd):
                pool.wait_ge(a_xT[3].sem, a_xT[3].at(n))
                pool.wait_ge(a_x3h.sem, a_x3h.at(n))
                tt(x3T_lo[odd][:], xT[3][:], x3T_hi[odd][:].bitcast(F32), ALU.subtract).then_inc(g_x3l.sem, 1)

            def e_norm(n):
                pool.wait_ge(g_ln[3].sem, g_ln[3].at(n))
                tt(centered[:], res[3][:], mean[3][:].unsqueeze(2).broadcast_to([P, TILES, P]), ALU.subtract).then_inc(g_cent.sem, 1)
                pool.wait_ge(g_cent.sem, g_cent.at(n))
                if started(n):
                    pool.wait_ge(x_st.sem, x_st.at(n - 1))
                tt(x4[:], centered[:], rstd[3][:].unsqueeze(2).broadcast_to([P, TILES, P]), ALU.mult).then_inc(g_x4.sem, 1)

            def turn(i, odd):
                a, bc, r, d, e = live(i), live(i - 1), live(i - 2), live(i - 3), live(i - 4)
                if e: ln_of(3, i - 4)
                if bc: b_norm(i - 1)
                if a: a_rope(i)
                if r: x3_lo(i - 2, odd)
                if bc: ln_of(1, i - 1)
                if e: e_norm(i - 4)
                if bc: x2_bias(i - 1)
                if a: a_rd(i)
                if r: r_split(i - 2)
                if a: a_mix(i)
                if a: ln_of(0, i)
                if bc: ln_of(2, i - 1)

            for i in range(LEAD):
                turn(i, i % 2)
            with pool.Fori(0, loops) as k:
                turn(2 * k + LEAD, 0)
                turn(2 * k + LEAD + 1, 1)
            for i in range(blocks, turns):
                turn(i, i % 2)


def _constants():
    c = {}
    inv_freq = (1.0 / np.float32(10000.0) ** (np.arange(0, HD, 2, dtype=np.float32) / np.float32(HD))).astype(np.float32)
    freqs = np.arange(SEQ, dtype=np.float32)[:, None] * inv_freq[None, :]
    emb = np.concatenate([freqs, freqs], axis=-1)
    sin, cos = np.sin(emb).astype(np.float32), np.cos(emb).astype(np.float32)
    sin = np.concatenate([-sin[:, :HD // 2], sin[:, HD // 2:]], axis=-1)
    spread = lambda t: np.tile(t.reshape(2, P, 1, HD), (1, 1, 2 * HEADS, 1)).transpose(1, 0, 2, 3).reshape(P, BLOCK)
    c["cos"], c["sin"] = spread(cos), spread(sin)
    d = np.arange(P)
    c["hmask"] = (d[:, None] // HD == d[None, :] // HD) * np.float32(A_SCALE)
    c["hmask8"] = (d[:, None] // HD == np.arange(HEADS)[None, :]) * np.float32(A_SCALE)
    c["ident"] = np.eye(P)
    c["causal"] = np.where(d[None, :] > d[:, None], np.float32(MASKED), 0.0)
    c["order"] = np.tile(np.arange(4, 0, -1), (P, 1))
    g = np.arange(GROUPS)
    c["before"] = np.tile((g[None, :] < g[:, None]).reshape(1, -1), (P, 1))
    c["ones"] = np.ones((P, P))
    c["sel_head"] = np.tile(np.arange(HEADS), 3)[:, None] == d[None, :] // HD
    f = np.arange(CHUNKS * P)
    c["sel_exp"] = np.tile(np.arange(EXPERTS), 3)[:, None] == f[None, :] // EF
    c["carry"] = np.tile(np.arange(TILES * EXPERTS) % EXPERTS != 0, (P, 1))
    for name, value in (("zero", 0.0), ("half", 0.5), ("neg_half", -0.5), ("quarter", 0.25), ("inv_p", 1.0 / P),
                        ("eps", EPS)):
        lo, up = WHOLE_COLS[name]
        c[name] = np.full((P, up - lo), value)
    return c


def _fill(width, table, parts):
    out = np.zeros((P, width), np.float32)
    for name, a in parts.items():
        lo, up = table[name]
        out[:a.shape[0], lo:lo + a.shape[1]] = a
    return out


def kernel(**inputs):
    import concourse.bacc as _bacc
    from concourse.bass_utils import run_bass_kernel_spmd as _run

    w = {k: np.asarray(v) for k, v in inputs.items()}
    x = np.ascontiguousarray(w["L0_attn_hidden_states"])
    ffn = lambda a: w["L0_ffn_" + a]
    moe = lambda a: w["L1_ffn_" + a]
    hidden = lambda e, s: np.concatenate([moe(e).reshape(EXPERTS * EF, P), moe(s)], axis=0).T
    down = np.concatenate([moe("w2_e").transpose(0, 2, 1).reshape(EXPERTS * EF, P), moe("w2_s").T], axis=0)
    rows = lambda a: np.repeat(a.reshape(1, -1), P, axis=0)
    split = {
        "qk": np.concatenate([w["L0_attn_Wq"], w["L0_attn_Wk"]], axis=0).T, "v": w["L0_attn_Wv"].T, "g": w["L0_attn_Wg"].T,
        "base": ffn("W").T, "proj": ffn("Wp").T, "down": np.concatenate([ffn(f"Wd{i}") for i in range(4)], axis=0).T,
        "cq": w["L1_attn_W"][:, 0:P], "ck": w["L1_attn_W"][:, P:2 * P], "cv": w["L1_attn_W"][:, 2 * P:3 * P],
        "gate": moe("w_gate").T, "w1": hidden("w1_e", "w1_s"), "w3": hidden("w3_e", "w3_s"),
    }
    whole = _constants()
    whole.update({
        "wo": w["L0_attn_Wo"].T, "w2": down.reshape(ALLCH, P, P).transpose(1, 0, 2).reshape(P, ALLCH * P),
        "taps": w["L0_attn_lepe_w"].reshape(P, TAPS), "tapb": w["L0_attn_lepe_b"].reshape(P, 1),
        "bp": rows(ffn("bp")), "bcq": w["L1_attn_b"][0:P].reshape(P, 1), "bck": w["L1_attn_b"][P:2 * P].reshape(P, 1),
        "bcv": rows(w["L1_attn_b"][2 * P:3 * P]), "temp": rows(ffn("temp")), "wp": ffn("Wp"), "sim": ffn("sim"),
        "bprep": np.repeat(ffn("bp").reshape(PROJ, 1), P, axis=1),
        "up": np.concatenate([ffn(f"Wu{i}").T for i in range(4)], axis=0),
    })
    arrays = {
        "x": x.reshape(-1, P),
        "w_split": _fill(N_SPLIT, SPLIT_COLS, split),
        "w_whole": _fill(N_WHOLE, WHOLE_COLS, whole),
    }
    nc = _bacc.Bacc("TRN2", target_bir_lowering=False, num_devices=1)
    args = [nc.dram_tensor(name, a.shape, F32, kind="ExternalInput").ap() for name, a in arrays.items()]
    out = nc.dram_tensor("out", arrays["x"].shape, F32, kind="ExternalOutput").ap()
    build(nc, *args, out)
    r = _run(nc, [arrays], core_ids=[0])
    return r.results[0]["out"].reshape(x.shape)
```

```python
from contextlib import ExitStack

import numpy as np

import concourse.bass as bass
from concourse import mybir

ALU = mybir.AluOpType
ACT = mybir.ActivationFunctionType
AX = mybir.AxisListType
F32 = mybir.dt.float32
F32R = mybir.dt.float32r
BF16 = mybir.dt.bfloat16

P = 128
SEQ = 256
TILES = 4
BLOCK = TILES * P
SEQS = BLOCK // SEQ
HEADS, HD = 8, 16
TAPS = 5
PROJ, RANKS = 32, (1, 2, 4, 8)
RANK_SUM, RANK_PAD = sum(RANKS), 16
SUB = 32
EXPERTS, GROUPS, EF = 16, 4, 64
CHUNKS = EXPERTS * EF // P
ALLCH = CHUNKS + 1
EPS = 1e-5
CLAMP_MAX = float(np.log(1.0 / 0.01))
A_SCALE = HD ** -0.5
C_SCALE = P ** -0.5
MASKED = -9.0e15

WEIGHT_COLS = {}
CONST_COLS = {}


def _place(table, parts):
    at = 0
    for name, width in parts:
        table[name] = (at, at + width)
        at += width
    return at


N_WEIGHT = _place(WEIGHT_COLS, [("w1", ALLCH * P), ("w3", ALLCH * P), ("qk", 2 * P), ("g", P), ("v", P), ("base", P),
                                ("proj", PROJ), ("logit", len(RANKS)), ("down", RANK_PAD), ("cq", P), ("ck", P),
                                ("cv", P), ("gate", EXPERTS)])
W_LATE, W_SPLIT = WEIGHT_COLS["w3"][1], WEIGHT_COLS["g"][1]
W_SMALL = WEIGHT_COLS["down"][1] - WEIGHT_COLS["proj"][0]
N_CONST = _place(CONST_COLS, [("w2", ALLCH * P), ("sel_exp", CHUNKS * P), ("ident", P), ("wo", P), ("cos", BLOCK),
                              ("sin", BLOCK), ("hmask", P), ("hmask8", HEADS), ("taps", TAPS), ("tapb", 1),
                              ("bp", PROJ), ("bcq", 1), ("bck", 1), ("bcv", P), ("causal", P), ("order", len(RANKS)),
                              ("before", GROUPS * GROUPS), ("temp", 1), ("wp", P), ("sim", len(RANKS)),
                              ("bprep", P), ("ones", P), ("up", P), ("zero", TILES * EXPERTS),
                              ("carry", TILES * EXPERTS), ("half", TILES), ("neg_half", TILES), ("quarter", TILES),
                              ("inv_p", TILES), ("eps", TILES)])
C_LATE = CONST_COLS["sel_exp"][1]


def n_is(n, least):
    return not isinstance(n, int) or n >= least


class Signal:

    def __init__(self, sem, per):
        self.sem, self.per = sem, per

    def at(self, n, k=None):
        return n * self.per + (self.per if k is None else k)


def started(n):
    return not (isinstance(n, int) and n == 0)


def build(nc, x_dram, weight_dram, whole_dram, out_dram):
    blocks = x_dram.shape[0] // BLOCK
    LEAD = 6
    loops = (blocks - LEAD) // 2
    turns = blocks + 4
    assert blocks % 2 == 0 and loops > 0

    def live(n):
        return not isinstance(n, int) or 0 <= n < blocks

    x_view = x_dram.rearrange("(n t p) d -> n p t d", t=TILES, p=P)
    out_view = out_dram.rearrange("(n t p) d -> n p t d", t=TILES, p=P)

    with ExitStack() as ctx:
        def sb(name, shape, dt=F32):
            return ctx.enter_context(nc.sbuf_tensor(name, shape, dt))

        def sig(name, per=1):
            return Signal(ctx.enter_context(nc.semaphore(name)), per)

        bank = [ctx.enter_context(nc.psum_tensor(f"bank{i}", [P, BLOCK], F32)) for i in range(8)]
        GB, UB, CB, YB = bank[0:4]
        A0, A1 = bank[4:6]
        B0, B1 = bank[6:8]

        w_raw = sb("w_raw", [P, N_WEIGHT])
        w_hi = sb("w_hi", [P, W_SPLIT], F32R)
        w_lo = sb("w_lo", [P, W_SPLIT], F32R)
        whole = sb("whole", [P, N_CONST])

        def hi(name, a=0, b=None):
            lo_, up_ = WEIGHT_COLS[name]
            return w_hi[:, lo_ + a:(up_ if b is None else lo_ + b)]

        def lo(name, a=0, b=None):
            lo_, up_ = WEIGHT_COLS[name]
            return w_lo[:, lo_ + a:(up_ if b is None else lo_ + b)]

        def const(name, parts=P):
            a, b = CONST_COLS[name]
            return whole[0:parts, a:b]

        ident = const("ident")
        ident_b = sb("ident_b", [P, P], BF16)
        causal_b = sb("causal_b", [P, P], BF16)
        sel_exp_b = sb("sel_exp_b", [3 * EXPERTS, CHUNKS * P], BF16)
        clamp_t = sb("clamp_t", [P, 1])
        escale = sb("escale", [P, 1])
        sim_sq = sb("sim_sq", [PROJ, 4])
        sim_n2 = sb("sim_n2", [PROJ, 4])
        sim_rn = sb("sim_rn", [PROJ, 4])
        sim_s = sb("sim_s", [PROJ, 4])
        bp_logit = sb("bp_logit", [P, 4])
        bcq_s = sb("bcq_s", [P, 1])

        x_in = sb("x_in", [P, 2, TILES, P])
        xT = [sb(f"x{k}T", [P, BLOCK]) for k in range(4)]
        x0T_hi = sb("x0T_hi", [P, BLOCK], F32R)
        x0T_lo = sb("x0T_lo", [P, BLOCK], F32R)
        x3T_hi = [sb(f"x3T_hi{i}", [P, BLOCK], F32R) for i in range(2)]
        x3T_lo = [sb(f"x3T_lo{i}", [P, BLOCK], F32R) for i in range(2)]
        x3 = [sb(f"x3_{i}", [P, TILES, P]) for i in range(2)]
        rope_c = sb("rope_c", [P, 2, BLOCK])
        rope_s = sb("rope_s", [P, 2, BLOCK])
        qk = sb("qk", [P, TILES, 2 * P])
        v_one = sb("v_one", [P, TILES, P + 1])
        gT = sb("gT", [P, BLOCK])
        kv_m = sb("kv_m", [P, SEQS, P])
        ks_m = sb("ks_m", [P, SEQS, HEADS])
        v_sum = sb("v_sum", [P, SEQS])
        qT = sb("qT", [P, BLOCK])
        vT = sb("vT", [P, SEQS, SEQ + 4])
        conv = sb("conv", [P, SEQS, SEQ])
        den = sb("den", [P, TILES * HEADS])
        rden = sb("rden", [P, TILES, HEADS])
        rden_x = sb("rden_x", [P, TILES, P])
        numT = sb("numT", [P, BLOCK])
        attT = sb("attT", [P, BLOCK])
        mixT = sb("mixT", [P, BLOCK])
        oT = sb("oT", [P, BLOCK])
        res = [sb(f"res{k}", [P, TILES, P]) for k in range(4)]
        stats = [sb(f"stats{k}", [P, TILES, 6]) for k in range(4)]
        moment = [sb(f"moment{k}", [P, 8, TILES]) for k in range(4)]
        mean = [sb(f"mean{k}", [P, TILES]) for k in range(4)]
        shift = sb("shift", [P, TILES])
        rstd = [sb(f"rstd{k}", [P, TILES]) for k in range(4)]
        x1, x2, x4 = (sb(name, [P, TILES, P]) for name in ("x1", "x2", "x4"))
        x2_b = sb("x2_b", [P, TILES, P])
        centered = sb("centered", [P, TILES, P])
        proj = sb("proj", [P, TILES, PROJ])
        proj_sq = sb("proj_sq", [P, TILES, PROJ])
        proj_n2 = sb("proj_n2", [P, TILES])
        proj_n2c = sb("proj_n2c", [P, TILES])
        proj_rn = sb("proj_rn", [P, TILES])
        lg_b = sb("lg_b", [P, TILES, 4])
        lg = sb("lg", [P, TILES, 4])
        lg_max = sb("lg_max", [P, TILES])
        lg_s = sb("lg_s", [P, TILES, 4])
        lg_e = sb("lg_e", [P, TILES, 4])
        lg_sum = sb("lg_sum", [P, TILES])
        lw_max = sb("lw_max", [P, TILES])
        cand = sb("cand", [P, TILES, 4])
        cand_max = sb("cand_max", [P, TILES])
        first = sb("first", [P, TILES, 4])
        ret = sb("ret", [P, TILES, 4])
        small = sb("small", [P, TILES, W_SMALL])
        down_m = sb("down_m", [P, TILES, RANK_SUM])
        down_x = sb("down_x", [P, TILES, 3, SUB])
        downT = sb("downT", [3 * SUB, BLOCK], F32R)
        up_x = sb("up_x", [3 * SUB, P], F32R)
        cqT = sb("cqT", [P, BLOCK])
        ckT = sb("ckT", [P, BLOCK])
        cv = sb("cv", [P, TILES, P])
        neg_max = sb("neg_max", [P, TILES])
        prob = sb("prob", [P, SEQS, 3 * P])
        row_sum = sb("row_sum", [P, TILES])
        row_inv = sb("row_inv", [P, TILES])
        probT = sb("probT", [P, SEQS, 3 * P])
        ez = sb("ez", [P, TILES * EXPERTS])
        ez1 = sb("ez1", [P, TILES * EXPERTS])
        score = sb("score", [P, TILES, EXPERTS])
        pair_hi = sb("pair_hi", [P, TILES * 8])
        pair_sum = sb("pair_sum", [P, TILES * 8])
        cross = sb("cross", [P, TILES * 4])
        inner = sb("inner", [P, TILES * 4])
        gscore = sb("gscore", [P, TILES, GROUPS])
        g_diff = sb("g_diff", [P, TILES, GROUPS, GROUPS])
        g_tie = sb("g_tie", [P, TILES, GROUPS, GROUPS])
        g_beat = sb("g_beat", [P, TILES, GROUPS, GROUPS])
        g_rank = sb("g_rank", [P, TILES, GROUPS])
        penalty = sb("penalty", [P, TILES, GROUPS])
        masked = sb("masked", [P, TILES, EXPERTS])
        top8 = sb("top8", [P, TILES, 8])
        above = sb("above", [P, TILES, EXPERTS])
        n_above = sb("n_above", [P, TILES])
        equal = sb("equal", [P, TILES, EXPERTS])
        count = sb("count", [P, TILES, EXPERTS])
        place = sb("place", [P, TILES, EXPERTS])
        tied = sb("tied", [P, TILES, EXPERTS])
        chosen = sb("chosen", [P, TILES, EXPERTS])
        wsel = sb("wsel", [P, TILES, EXPERTS])
        wsum = sb("wsum", [P, TILES])
        wsum_e = sb("wsum_e", [P, TILES])
        winv = sb("winv", [P, TILES])
        comb = sb("comb", [P, TILES, EXPERTS])
        comb_r = sb("comb_r", [P, TILES, EXPERTS])
        comb_b = sb("comb_b", [P, TILES, 6, EXPERTS], BF16)
        silu = sb("silu", [P, 2, BLOCK])
        gu = sb("gu", [P, 2, BLOCK])
        hid = sb("hid", [P, 2, BLOCK])
        combT = sb("combT", [3 * EXPERTS, BLOCK], BF16)
        yT = sb("yT", [P, BLOCK])

        w_in, k_in, late_in, x_st = sig("w_in"), sig("k_in"), sig("late_in"), sig("x_st", 16)
        x_ld = [sig(f"x_ld{i}", 16) for i in range(2)]
        setup_v, setup_a, setup_p, setup_g = sig("setup_v"), sig("setup_a"), sig("setup_p"), sig("setup_g")
        p_xT = [sig(f"p_x{k}T") for k in range(4)]
        a_xT = [sig(f"a_x{k}T") for k in range(4)]
        a_x0h, g_x0l, a_x3h, g_x3l = sig("a_x0h"), sig("g_x0l"), sig("a_x3h"), sig("g_x3l")
        p_qk, p_v, p_g, p_kv = sig("p_qk", 2), sig("p_v"), sig("p_g"), sig("p_kv")
        p_qT, p_vT, p_den, p_num = sig("p_qT"), sig("p_vT"), sig("p_den"), sig("p_num")
        p_rd, p_y = sig("p_rd"), sig("p_y")
        v_rope, g_qk, a_v, a_g = sig("v_rope", 6), sig("g_qk", 2), sig("a_v"), sig("a_g")
        v_kv, a_qT, a_vT, a_tap, v_conv = sig("v_kv", 2), sig("a_qT"), sig("a_vT", SEQS), sig("a_tap"), sig("v_conv", TAPS - 1)
        v_den, v_rden, g_rd, a_num = sig("v_den"), sig("v_rden"), sig("g_rd"), sig("a_num", SEQS)
        v_att, g_mix, v_oT = sig("v_att"), sig("g_mix"), sig("v_oT")
        v_res = [sig(f"v_res{k}", TILES if k == 2 else 1) for k in range(4)]
        v_st = [sig(f"v_st{k}", TILES) for k in range(4)]
        g_ln = [sig(f"g_ln{k}", 11 if k == 1 else 10) for k in range(4)]
        v_x1, a_x2, g_x3 = sig("v_x1", TILES), sig("a_x2", TILES), sig("g_x3", 2)
        g_cent, g_x4 = sig("g_cent"), sig("g_x4")
        p_small, p_dnT, p_up = sig("p_small"), sig("p_dnT"), sig("p_up")
        B_NORM2, B_LOGITS = 5, 8
        v_b, g_b, a_b, v_down, a_dnT = sig("v_b", 14), sig("g_b"), sig("a_b"), sig("v_down", len(RANKS) + 2), sig("a_dnT")
        g_x2b, a_small = sig("g_x2b"), sig("a_small")
        p_cq, p_ck, p_cv, p_s, p_pT, p_av = sig("p_cq"), sig("p_ck"), sig("p_cv"), sig("p_s", 2), sig("p_pT", 2), sig("p_av")
        a_cq, a_ck, a_cv, v_max, a_exp, a_pT, v_rinv = (sig("a_cq"), sig("a_ck"), sig("a_cv"), sig("v_max", 4),
                                                        sig("a_exp", 4), sig("a_pT", 2), sig("v_rinv"))
        R_MASKED, R_TOP = 13, 17
        p_gate, a_ez, v_r, g_c, p_cT, a_cT = sig("p_gate"), sig("a_ez"), sig("v_r", 29), sig("g_c", 4), sig("p_cT"), sig("a_cT")
        p_G, p_U, p_C, p_w2, p_yT = sig("p_G", ALLCH), sig("p_U", ALLCH), sig("p_C", CHUNKS), sig("p_w2", ALLCH), sig("p_yT")
        a_silu, v_gu, v_hid, a_y = sig("a_silu", ALLCH), sig("v_gu", ALLCH), sig("v_hid", CHUNKS), sig("a_y")

        block = ctx.enter_context(nc.Block())

        @block.sync
        def _(sp):
            nc.sync.dma_start(whole[:, C_LATE:], whole_dram[:, C_LATE:]).then_inc(k_in.sem, 16)
            nc.sync.dma_start(x_in[:, 0], x_view[0]).then_inc(x_ld[0].sem, 16)
            nc.sync.dma_start(w_raw[:, W_LATE:], weight_dram[:, W_LATE:]).then_inc(w_in.sem, 16)
            nc.sync.dma_start(x_in[:, 1], x_view[1]).then_inc(x_ld[1].sem, 16)
            nc.sync.dma_start(w_raw[:, 0:W_LATE], weight_dram[:, 0:W_LATE]).then_inc(late_in.sem, 16)
            nc.sync.dma_start(whole[:, 0:C_LATE], whole_dram[:, 0:C_LATE]).then_inc(late_in.sem, 16)

            def load_after(n, half):
                sp.wait_ge(v_res[0].sem, v_res[0].at(n))
                nc.sync.dma_start(x_in[:, half], x_view[n + 2]).then_inc(x_ld[half].sem, 16)

            def store(n):
                sp.wait_ge(g_x4.sem, g_x4.at(n))
                nc.sync.dma_start(out_view[n], x4[:]).then_inc(x_st.sem, 16)

            for n in range(4):
                load_after(n, n % 2)
            with sp.Fori(0, blocks // 2 - 3) as k:
                store(2 * k)
                load_after(2 * k + 4, 0)
                store(2 * k + 1)
                load_after(2 * k + 5, 1)
            for n in range(blocks - 6, blocks):
                store(n)
            sp.wait_ge(x_st.sem, x_st.at(blocks - 1))

        @block.tensor
        def _(pe):
            mm = nc.tensor.matmul

            def mm3(out, wh, wl, mh, ml):
                mm(out, wh, mh, start=True, stop=False)
                mm(out, wh, ml, start=False, stop=False)
                return mm(out, wl, mh, start=False, stop=True)

            def tile(ap, t):
                return ap[:, t * P:(t + 1) * P]

            def transpose_tiles(out, src, eye, parts=P):
                for t in range(TILES):
                    last = nc.tensor.transpose(out[0:parts, t * P:(t + 1) * P], src(t), eye)
                return last

            def raw(name, a=0, b=None):
                first, end = WEIGHT_COLS[name]
                return w_raw[:, first + a:(end if b is None else first + b)]

            pe.wait_ge(k_in.sem, 16)
            pe.wait_ge(setup_v.sem, 1)
            mm(A0[0:PROJ, 0:4], const("ones", PROJ)[:, 0:PROJ], sim_sq[:], start=True, stop=True).then_inc(setup_p.sem, 1)
            pe.wait_ge(setup_v.sem, 7)
            mm(A1[:, 0:4], const("wp", PROJ), sim_s[:], start=True, stop=True)
            mm(B0[:, 0:4], const("bprep", PROJ), sim_s[:], start=True, stop=True).then_inc(setup_p.sem, 1)
            pe.wait_ge(setup_v.sem, 11)
            pe.wait_ge(setup_a.sem, 4)

            def a_xT_(n, half, load):
                pe.wait_ge(x_ld[half].sem, x_ld[half].at(load))
                if n_is(n, 3):
                    pe.wait_ge(a_cT.sem, a_cT.at(n - 3))
                elif started(n):
                    pe.wait_ge(a_num.sem, a_num.at(n - 1))
                transpose_tiles(A0, lambda t: x_in[:, half, t], ident).then_inc(p_xT[0].sem, 1)

            def a_v_(n):
                pe.wait_ge(a_xT[0].sem, a_xT[0].at(n))
                if started(n):
                    pe.wait_ge(v_res[0].sem, v_res[0].at(n - 1))
                for t in range(TILES):
                    last = mm(tile(A1, t), tile(xT[0], t), raw("v"), start=True, stop=True)
                last.then_inc(p_v.sem, 1)

            def a_qk(n):
                pe.wait_ge(g_x0l.sem, g_x0l.at(n))
                for h, b in ((0, A0), (1, A1)):
                    if h == 1:
                        pe.wait_ge(a_v.sem, a_v.at(n))
                    for i in range(2):
                        xh, xl = tile(x0T_hi, 2 * h + i), tile(x0T_lo, 2 * h + i)
                        out = b[:, i * 2 * P:(i + 1) * 2 * P]
                        mm(out, xh, hi("qk"), start=True, stop=False)
                        mm(out, xh, lo("qk"), start=False, stop=False)
                        last = mm(out, xl, hi("qk"), start=False, stop=True)
                    last.then_inc(p_qk.sem, 1)

            def a_g_(n):
                pe.wait_ge(v_rope.sem, v_rope.at(n, 3))
                mm3(A0[:], hi("g"), lo("g"), x0T_hi[:], x0T_lo[:]).then_inc(p_g.sem, 1)

            def a_kv(n):
                pe.wait_ge(g_qk.sem, g_qk.at(n))
                pe.wait_ge(a_vT.sem, a_vT.at(n))
                for s in range(SEQS):
                    for i in range(2):
                        last = mm(A1[:, s * SEQ:s * SEQ + P + 1], qk[:, 2 * s + i, P:2 * P], v_one[:, 2 * s + i, :],
                           start=i == 0, stop=i == 1)
                last.then_inc(p_kv.sem, 1)

            def a_vT_(n):
                pe.wait_ge(a_v.sem, a_v.at(n))
                pe.wait_ge(v_rope.sem, v_rope.at(n))
                transpose_tiles(A1, lambda t: v_one[:, t, 0:P], ident).then_inc(p_vT.sem, 1)

            def a_qT_(n):
                pe.wait_ge(a_g.sem, a_g.at(n))
                transpose_tiles(A0, lambda t: qk[:, t, 0:P], ident).then_inc(p_qT.sem, 1)

            def a_den(n):
                pe.wait_ge(a_qT.sem, a_qT.at(n))
                pe.wait_ge(v_kv.sem, v_kv.at(n))
                for t in range(TILES):
                    last = mm(A1[:, t * HEADS:(t + 1) * HEADS], tile(qT, t), ks_m[:, t // 2, :], start=True, stop=True)
                last.then_inc(p_den.sem, 1)

            def a_num_(n):
                for s in range(SEQS):
                    last = mm(A0[:, s * SEQ:(s + 1) * SEQ], kv_m[:, s, :], qT[:, s * SEQ:(s + 1) * SEQ], start=True, stop=True)
                last.then_inc(p_num.sem, 1)

            def a_rd(n):
                pe.wait_ge(g_rd.sem, g_rd.at(n))
                transpose_tiles(A1, lambda t: rden_x[:, t], ident).then_inc(p_rd.sem, 1)

            def a_out(n):
                pe.wait_ge(v_oT.sem, v_oT.at(n))
                for t in range(TILES):
                    last = mm(tile(A1, t), tile(oT, t), const("wo"), start=True, stop=True)
                last.then_inc(p_y.sem, 1)

            def b_xT(n):
                pe.wait_ge(v_x1.sem, v_x1.at(n))
                if started(n):
                    pe.wait_ge(a_pT.sem, a_pT.at(n - 1, 1))
                transpose_tiles(B0, lambda t: x1[:, t], ident).then_inc(p_xT[1].sem, 1)

            def b_small(n):
                pe.wait_ge(a_xT[1].sem, a_xT[1].at(n))
                a, b = WEIGHT_COLS["proj"][0], WEIGHT_COLS["down"][1]
                w = b - a
                for t in range(TILES):
                    last = mm(B0[:, t * w:(t + 1) * w], tile(xT[1], t), w_raw[:, a:b], start=True, stop=True)
                last.then_inc(p_small.sem, 1)

            def b_dnT(n):
                pe.wait_ge(v_down.sem, v_down.at(n))
                transpose_tiles(B0, lambda t: down_x[:, t].rearrange("p a r -> p (a r)"), ident, parts=3 * SUB).then_inc(p_dnT.sem, 1)

            def b_up(n):
                pe.wait_ge(a_dnT.sem, a_dnT.at(n))
                if started(n):
                    pe.wait_ge(a_ez.sem, a_ez.at(n - 1))
                for t in range(TILES):
                    mm(tile(B1, t), tile(xT[1], t), raw("base"), start=True, stop=False)
                    last = mm(tile(B1, t), tile(downT, t), up_x[:], start=False, stop=True)
                last.then_inc(p_up.sem, 1)

            def c_xT(n):
                pe.wait_ge(a_x2.sem, a_x2.at(n))
                transpose_tiles(B0, lambda t: x2[:, t], ident).then_inc(p_xT[2].sem, 1)

            def c_project(n):
                pe.wait_ge(a_xT[2].sem, a_xT[2].at(n))
                mm(B1[:], raw("cq"), xT[2][:], start=True, stop=True).then_inc(p_cq.sem, 1)
                mm(B0[:], raw("ck"), xT[2][:], start=True, stop=True).then_inc(p_ck.sem, 1)

            def c_value(n):
                pe.wait_ge(a_cq.sem, a_cq.at(n))
                for t in range(TILES):
                    last = mm(tile(B1, t), tile(xT[2], t), raw("cv"), start=True, stop=True)
                last.then_inc(p_cv.sem, 1)

            def c_scores(n):
                pe.wait_ge(a_ck.sem, a_ck.at(n))
                for s, b in ((0, B0), (1, B1)):
                    if s == 1:
                        pe.wait_ge(a_cv.sem, a_cv.at(n))
                    q0, q1 = tile(cqT, 2 * s), tile(cqT, 2 * s + 1)
                    k0, k1 = tile(ckT, 2 * s), tile(ckT, 2 * s + 1)
                    mm(b[:, 0:P], ident_b[:], causal_b[:], start=True, stop=False)
                    mm(b[:, 0:P], q0, k0, start=False, stop=True)
                    mm(b[:, P:2 * P], q1, k0, start=True, stop=True)
                    mm(b[:, 2 * P:3 * P], ident_b[:], causal_b[:], start=True, stop=False)
                    mm(b[:, 2 * P:3 * P], q1, k1, start=False, stop=True).then_inc(p_s.sem, 1)

            def c_pT(n):
                for s, b in ((0, B0), (1, B1)):
                    pe.wait_ge(a_exp.sem, a_exp.at(n, 2 * s + 2))
                    for i in range(3):
                        last = nc.tensor.transpose(b[:, i * P:(i + 1) * P], prob[:, s, i * P:(i + 1) * P], ident)
                    last.then_inc(p_pT.sem, 1)

            def c_av(n):
                pe.wait_ge(a_pT.sem, a_pT.at(n))
                for s in range(SEQS):
                    mm(tile(B1, 2 * s), probT[:, s, 0:P], cv[:, 2 * s], start=True, stop=True)
                    mm(tile(B1, 2 * s + 1), probT[:, s, P:2 * P], cv[:, 2 * s], start=True, stop=False)
                    last = mm(tile(B1, 2 * s + 1), probT[:, s, 2 * P:3 * P], cv[:, 2 * s + 1], start=False, stop=True)
                last.then_inc(p_av.sem, 1)

            def r_xT(n, odd):
                pe.wait_ge(g_x3.sem, g_x3.at(n))
                transpose_tiles(B1, lambda t: x3[odd][:, t], ident).then_inc(p_xT[3].sem, 1)

            def r_gate(n):
                pe.wait_ge(a_x3h.sem, a_x3h.at(n))
                for t in range(TILES):
                    last = mm(B1[:, t * EXPERTS:(t + 1) * EXPERTS], tile(xT[3], t), raw("gate"), start=True, stop=True)
                last.then_inc(p_gate.sem, 1)

            def d_cT(n, behind):
                pe.wait_ge(g_c.sem, g_c.at(n))
                if behind:
                    pe.wait_ge(a_num.sem, a_num.at(n + 2))
                transpose_tiles(A0[:].bitcast(BF16), lambda t: comb_b[:, t].rearrange("p a e -> p (a e)"), ident_b[:],
                                parts=6 * EXPERTS).then_inc(p_cT.sem, 1)

            def d_hidden(n, odd, c):
                xh, xl = x3T_hi[odd], x3T_lo[odd]
                if c == 0:
                    pe.wait_ge(g_x3l.sem, g_x3l.at(n))
                if c > 0 or started(n):
                    pe.wait_ge(a_silu.sem, a_silu.at(n, c))
                w = c * P, (c + 1) * P
                mm3(GB[:], hi("w1", *w), lo("w1", *w), xh[:], xl[:]).then_inc(p_G.sem, 1)
                if c > 0 or started(n):
                    pe.wait_ge(v_gu.sem, v_gu.at(n, c))
                mm3(UB[:], hi("w3", *w), lo("w3", *w), xh[:], xl[:]).then_inc(p_U.sem, 1)
                if 0 < c < CHUNKS:
                    d_spread(n, c)

            def d_spread(n, c):
                if c == 0:
                    pe.wait_ge(a_cT.sem, a_cT.at(n))
                if c > 0 or started(n):
                    pe.wait_ge(v_hid.sem, v_hid.at(n, c))
                mm(CB[:], sel_exp_b[:, c * P:(c + 1) * P], combT[:], start=True, stop=True).then_inc(p_C.sem, 1)

            def d_down(n, c):
                if c < CHUNKS:
                    pe.wait_ge(v_hid.sem, v_hid.at(n, c + 1))
                else:
                    pe.wait_ge(v_gu.sem, v_gu.at(n))
                if c == 0 and started(n):
                    pe.wait_ge(v_res[3].sem, v_res[3].at(n - 1))
                a = CONST_COLS["w2"][0] + c * P
                mm(YB[:], whole[:, a:a + P], hid[:, c % 2], start=c == 0, stop=c == CHUNKS).then_inc(p_w2.sem, 1)

            def d_yT(n):
                pe.wait_ge(a_y.sem, a_y.at(n))
                transpose_tiles(YB, lambda t: tile(yT, t), ident).then_inc(p_yT.sem, 1)

            def turn(i, odd, load=None):
                a, b, c, d, e = live(i), live(i - 1), live(i - 2), live(i - 3), live(i - 4)
                if d: d_hidden(i - 3, 1 - odd, 0)
                if d: d_cT(i - 3, live(i - 1))
                if c: c_scores(i - 2)
                if d: d_spread(i - 3, 0)
                if a: a_xT_(i, odd, load)
                if e: d_yT(i - 4)
                if d: d_hidden(i - 3, 1 - odd, 1)
                if d: d_down(i - 3, 0)
                if a: a_v_(i)
                if d: d_hidden(i - 3, 1 - odd, 2)
                if c: c_pT(i - 2)
                if a: a_qk(i)
                if d: d_down(i - 3, 1)
                if c: c_av(i - 2)
                if b: b_xT(i - 1)
                if d: d_hidden(i - 3, 1 - odd, 3)
                if b: b_small(i - 1)
                if a: a_g_(i)
                if d: d_down(i - 3, 2)
                if a: a_vT_(i)
                if d: d_hidden(i - 3, 1 - odd, 4)
                if d: d_down(i - 3, 3)
                if a: a_kv(i)
                if d: d_hidden(i - 3, 1 - odd, 5)
                if c: r_xT(i - 2, odd)
                if a: a_qT_(i)
                if d: d_down(i - 3, 4)
                if c: r_gate(i - 2)
                if b: b_dnT(i - 1)
                if d: d_hidden(i - 3, 1 - odd, 6)
                if a: a_den(i)
                if b: b_up(i - 1)
                if a: a_num_(i)
                if d: d_down(i - 3, 5)
                if d: d_hidden(i - 3, 1 - odd, 7)
                if a: a_rd(i)
                if d: d_down(i - 3, 6)
                if d: d_hidden(i - 3, 1 - odd, 8)
                if d: d_down(i - 3, 7)
                if d: d_down(i - 3, 8)
                if b: c_xT(i - 1)
                if a: a_out(i)
                if b: c_project(i - 1)
                if b: c_value(i - 1)

            for i in range(LEAD):
                if i == 3:
                    pe.wait_ge(late_in.sem, 2 * 16)
                    pe.wait_ge(setup_v.sem, 13)
                turn(i, i % 2, i // 2)
            with pe.Fori(0, loops) as k:
                turn(2 * k + LEAD, 0, k + LEAD // 2)
                turn(2 * k + LEAD + 1, 1, k + LEAD // 2)
            for i in range(blocks, turns):
                turn(i, i % 2)

        @block.scalar
        def _(act):
            fn = nc.scalar.activation
            act.wait_ge(k_in.sem, 16)
            act.wait_ge(setup_v.sem, 2)
            fn(escale[:], clamp_t[:], ACT.Exp).then_inc(setup_a.sem, 1)
            fn(bcq_s[:], const("bcq"), ACT.Copy, scale=C_SCALE).then_inc(setup_a.sem, 1)
            fn(up_x[:], const("up", 3 * SUB), ACT.Copy).then_inc(setup_a.sem, 1)
            act.wait_ge(w_in.sem, 16)
            fn(w_hi[:, W_LATE:], w_raw[:, W_LATE:W_SPLIT], ACT.Copy).then_inc(setup_a.sem, 1)
            act.wait_ge(setup_a.sem, 4)
            act.wait_ge(setup_v.sem, 11)

            def split_late():
                act.wait_ge(late_in.sem, 2 * 16)
                fn(w_hi[:, 0:W_LATE], w_raw[:, 0:W_LATE], ACT.Copy).then_inc(setup_a.sem, 1)

            def copy_xT(n, k, b):
                act.wait_ge(p_xT[k].sem, p_xT[k].at(n))
                fn(xT[k][:], b[:], ACT.Copy).then_inc(a_xT[k].sem, 1)

            def b_layer_norm(n):
                act.wait_ge(g_ln[1].sem, g_ln[1].at(n))
                for t in range(TILES):
                    fn(x2[:, t, :], res[1][:, t, :], ACT.Identity, scale=rstd[1][:, t:t + 1],
                       bias=shift[:, t:t + 1]).then_inc(a_x2.sem, 1)

            def x0_hi(n):
                act.wait_ge(p_xT[0].sem, p_xT[0].at(n))
                fn(x0T_hi[:], A0[:], ACT.Copy).then_inc(a_x0h.sem, 1)
                fn(xT[0][:], A0[:], ACT.Copy).then_inc(a_xT[0].sem, 1)

            def a_v_(n):
                act.wait_ge(p_v.sem, p_v.at(n))
                fn(v_one[:, :, 0:P], A1[:].rearrange("p (t d) -> p t d", t=TILES), ACT.Copy).then_inc(a_v.sem, 1)

            def a_g_(n):
                act.wait_ge(p_g.sem, p_g.at(n))
                fn(gT[:], A0[:], ACT.Copy).then_inc(a_g.sem, 1)

            def a_qT_(n):
                act.wait_ge(p_qT.sem, p_qT.at(n))
                fn(qT[:], A0[:], ACT.Copy).then_inc(a_qT.sem, 1)

            def a_vT_(n):
                act.wait_ge(p_vT.sem, p_vT.at(n))
                for s in range(SEQS):
                    fn(vT[:, s, 2:2 + SEQ], A1[:, s * SEQ:(s + 1) * SEQ], ACT.Identity,
                       accum_out=v_sum[:, s:s + 1]).then_inc(a_vT.sem, 1)
                act.wait_ge(a_vT.sem, a_vT.at(n))
                fn(conv[:], vT[:, :, 0:SEQ], ACT.Identity, scale=const("taps")[:, 0:1],
                   bias=const("tapb")).then_inc(a_tap.sem, 1)

            def a_numv(n):
                act.wait_ge(p_num.sem, p_num.at(n))
                act.wait_ge(a_vT.sem, a_vT.at(n))
                for s in range(SEQS):
                    fn(numT[:, s * SEQ:(s + 1) * SEQ], A0[:, s * SEQ:(s + 1) * SEQ], ACT.Identity,
                       bias=v_sum[:, s:s + 1]).then_inc(a_num.sem, 1)

            def b_exp(n):
                act.wait_ge(v_b.sem, v_b.at(n, B_LOGITS))
                fn(lg_e[:], lg_s[:], ACT.Exp).then_inc(a_b.sem, 1)

            def b_small(n):
                act.wait_ge(p_small.sem, p_small.at(n))
                fn(small[:].rearrange("p t c -> p (t c)"), B0[:, 0:TILES * W_SMALL], ACT.Copy).then_inc(a_small.sem, 1)

            def b_dnT(n):
                act.wait_ge(p_dnT.sem, p_dnT.at(n))
                fn(downT[:], B0[0:3 * SUB, :], ACT.Copy).then_inc(a_dnT.sem, 1)

            def c_qkv(n):
                act.wait_ge(p_cq.sem, p_cq.at(n))
                fn(cqT[:], B1[:], ACT.Identity, scale=C_SCALE, bias=bcq_s[:]).then_inc(a_cq.sem, 1)
                act.wait_ge(p_ck.sem, p_ck.at(n))
                fn(ckT[:], B0[:], ACT.Identity, bias=const("bck")).then_inc(a_ck.sem, 1)
                act.wait_ge(p_cv.sem, p_cv.at(n))
                fn(cv[:].rearrange("p t d -> p (t d)"), B1[:], ACT.Copy).then_inc(a_cv.sem, 1)

            def c_exp(n):
                for s, b in ((0, B0), (1, B1)):
                    act.wait_ge(v_max.sem, v_max.at(n, 2 * s + 2))
                    for i, (a, w) in enumerate(((0, P), (P, 2 * P))):
                        t = 2 * s + i
                        fn(prob[:, s, a:a + w], b[:, a:a + w], ACT.Exp, bias=neg_max[:, t:t + 1],
                           accum_out=row_sum[:, t:t + 1]).then_inc(a_exp.sem, 1)

            def c_pT(n):
                for s, b in ((0, B0), (1, B1)):
                    act.wait_ge(p_pT.sem, p_pT.at(n, s + 1))
                    fn(probT[:, s, :], b[:, 0:3 * P], ACT.Copy).then_inc(a_pT.sem, 1)

            def r_hi(n, odd):
                act.wait_ge(p_xT[3].sem, p_xT[3].at(n))
                fn(xT[3][:], B1[:], ACT.Copy).then_inc(a_xT[3].sem, 1)
                fn(x3T_hi[odd][:], B1[:], ACT.Copy).then_inc(a_x3h.sem, 1)

            def r_exp(n):
                act.wait_ge(p_gate.sem, p_gate.at(n))
                fn(ez[:], B1[:, 0:TILES * EXPERTS], ACT.Exp, scale=-1.0).then_inc(a_ez.sem, 1)

            def d_cT(n):
                act.wait_ge(p_cT.sem, p_cT.at(n))
                fn(combT[:], A0[:].bitcast(BF16)[0:3 * EXPERTS, 0:BLOCK], ACT.Copy).then_inc(a_cT.sem, 1)

            def d_silu(n, c):
                act.wait_ge(p_G.sem, p_G.at(n, c + 1))
                if c > 1 or started(n):
                    act.wait_ge(v_gu.sem, v_gu.at(n, max(c - 1, 0)))
                fn(silu[:, c % 2], GB[:], ACT.Silu).then_inc(a_silu.sem, 1)

            def d_y(n):
                act.wait_ge(p_w2.sem, p_w2.at(n))
                fn(yT[:], YB[:], ACT.Copy).then_inc(a_y.sem, 1)

            def turn(i, odd):
                a, b, c, d, e = live(i), live(i - 1), live(i - 2), live(i - 3), live(i - 4)
                if d: d_silu(i - 3, 0)
                if d: d_cT(i - 3)
                if a: x0_hi(i)
                if d: d_silu(i - 3, 1)
                if c: c_exp(i - 2)
                if a: a_v_(i)
                if d: d_silu(i - 3, 2)
                if c: c_pT(i - 2)
                if b: copy_xT(i - 1, 1, B0)
                if d: d_silu(i - 3, 3)
                if b: b_small(i - 1)
                if a: a_g_(i)
                if a: a_vT_(i)
                if d: d_silu(i - 3, 4)
                if b: b_exp(i - 1)
                if d: d_silu(i - 3, 5)
                if c: r_hi(i - 2, odd)
                if a: a_qT_(i)
                if c: r_exp(i - 2)
                if b: b_dnT(i - 1)
                if d: d_silu(i - 3, 6)
                if a: a_numv(i)
                if d: d_silu(i - 3, 7)
                if d: d_silu(i - 3, 8)
                if b: b_layer_norm(i - 1)
                if b: copy_xT(i - 1, 2, B0)
                if d: d_y(i - 3)
                if b: c_qkv(i - 1)

            for i in range(LEAD):
                if i == 1:
                    split_late()
                turn(i, i % 2)
            with act.Fori(0, loops) as k:
                turn(2 * k + LEAD, 0)
                turn(2 * k + LEAD + 1, 1)
            for i in range(blocks, turns):
                turn(i, i % 2)

        @block.vector
        def _(dve):
            tt, ts, stt, red = (nc.vector.tensor_tensor, nc.vector.tensor_scalar, nc.vector.scalar_tensor_tensor,
                                nc.vector.tensor_reduce)
            dve.wait_ge(k_in.sem, 16)
            sim = const("sim", PROJ)
            tt(sim_sq[:], sim, sim, ALU.mult).then_inc(setup_v.sem, 1)
            ts(clamp_t[:], const("temp"), CLAMP_MAX, None, ALU.min).then_inc(setup_v.sem, 1)
            nc.vector.tensor_copy(ident_b[:], ident).then_inc(setup_v.sem, 1)
            nc.vector.tensor_copy(causal_b[:], const("causal")).then_inc(setup_v.sem, 1)
            dve.wait_ge(setup_p.sem, 1)
            ts(sim_n2[:], A0[0:PROJ, 0:4], 1e-24, None, ALU.max).then_inc(setup_v.sem, 1)
            nc.vector.memset(down_x[:], 0.0).then_inc(setup_v.sem, 1)
            dve.wait_ge(setup_g.sem, 3)
            dve.wait_ge(setup_a.sem, 1)
            stt(sim_s[:], sim, escale[0:PROJ, 0:1], sim_rn[:], ALU.mult, ALU.mult).then_inc(setup_v.sem, 1)
            dve.wait_ge(w_in.sem, 16)
            dve.wait_ge(setup_a.sem, 4)
            tt(w_lo[:, W_LATE:], w_raw[:, W_LATE:W_SPLIT], w_hi[:, W_LATE:].bitcast(F32), ALU.subtract).then_inc(setup_v.sem, 1)
            dve.wait_ge(setup_p.sem, 2)
            a, b = WEIGHT_COLS["logit"]
            nc.vector.tensor_copy(w_raw[:, a:b], A1[:, 0:4]).then_inc(setup_v.sem, 1)
            nc.vector.tensor_copy(bp_logit[:], B0[:, 0:4]).then_inc(setup_v.sem, 1)
            tt(up_x[SUB:2 * SUB], const("up")[SUB:2 * SUB], up_x[SUB:2 * SUB].bitcast(F32), ALU.subtract).then_inc(setup_v.sem, 1)
            dve.wait_ge(setup_g.sem, 3 + 3)
            dve.wait_ge(setup_v.sem, 11)

            def split_late():
                dve.wait_ge(late_in.sem, 2 * 16)
                nc.vector.tensor_copy(sel_exp_b[:], const("sel_exp", 3 * EXPERTS)).then_inc(setup_v.sem, 1)
                dve.wait_ge(setup_a.sem, 5)
                tt(w_lo[:, 0:W_LATE], w_raw[:, 0:W_LATE], w_hi[:, 0:W_LATE].bitcast(F32), ALU.subtract).then_inc(setup_v.sem, 1)

            def heads(ap):
                return ap.rearrange("p (h d) -> p h d", d=HD)

            def tiles(ap):
                return ap.rearrange("p (t d) -> p t d", t=TILES)

            def per_tile(ap, w=4):
                return ap.unsqueeze(2).broadcast_to([P, TILES, w])

            def all_tiles(ap, w=4):
                return ap.unsqueeze(1).broadcast_to([P, TILES, w])

            def a_rope(n):
                half = HD // 2
                for h, b in ((0, A0), (1, A1)):
                    dve.wait_ge(p_qk.sem, p_qk.at(n, h + 1))
                    src, sin, out = heads(b[:]), heads(const("sin")), heads(rope_s[:, h])
                    tt(rope_c[:, h], b[:], const("cos"), ALU.mult).then_inc(v_rope.sem, 1)
                    tt(out[:, :, 0:half], src[:, :, half:HD], sin[:, :, 0:half], ALU.mult).then_inc(v_rope.sem, 1)
                    tt(out[:, :, half:HD], src[:, :, 0:half], sin[:, :, half:HD], ALU.mult).then_inc(v_rope.sem, 1)

            def a_kv(n):
                dve.wait_ge(p_kv.sem, p_kv.at(n))
                kv = A1[:].rearrange("p (s c) -> p s c", s=SEQS)
                tt(kv_m[:], kv[:, :, 0:P], const("hmask").unsqueeze(1).broadcast_to([P, SEQS, P]), ALU.mult).then_inc(v_kv.sem, 1)
                tt(ks_m[:], kv[:, :, P:P + 1].broadcast_to([P, SEQS, HEADS]),
                   const("hmask8").unsqueeze(1).broadcast_to([P, SEQS, HEADS]), ALU.mult).then_inc(v_kv.sem, 1)

            def a_den(n):
                dve.wait_ge(p_den.sem, p_den.at(n))
                ts(den[:], A1[:, 0:TILES * HEADS], float(SEQ), None, ALU.add).then_inc(v_den.sem, 1)
                dve.wait_ge(v_den.sem, v_den.at(n))
                nc.vector.reciprocal(rden[:].rearrange("p t h -> p (t h)"), den[:]).then_inc(v_rden.sem, 1)

            def a_att(n):
                dve.wait_ge(p_rd.sem, p_rd.at(n))
                dve.wait_ge(a_num.sem, a_num.at(n))
                tt(attT[:], numT[:], A1[:], ALU.mult).then_inc(v_att.sem, 1)

            def a_gate(n):
                dve.wait_ge(g_mix.sem, g_mix.at(n))
                dve.wait_ge(a_g.sem, a_g.at(n))
                tt(oT[:], mixT[:], gT[:], ALU.mult).then_inc(v_oT.sem, 1)

            def norm_stats(k, n):
                dve.wait_ge(v_res[k].sem, v_res[k].at(n))
                for t in range(TILES):
                    nc.vector.bn_stats(stats[k][:, t, :], res[k][:, t, :]).then_inc(v_st[k].sem, 1)

            def a_layer_norm(n):
                dve.wait_ge(g_ln[0].sem, g_ln[0].at(n))
                for t in range(TILES):
                    ts(x1[:, t, :], res[0][:, t, :], mean[0][:, t:t + 1], rstd[0][:, t:t + 1],
                       ALU.subtract, ALU.mult).then_inc(v_x1.sem, 1)

            def a_res(n, half):
                dve.wait_ge(p_y.sem, p_y.at(n))
                tt(res[0][:], x_in[:, half], tiles(A1[:]), ALU.add).then_inc(v_res[0].sem, 1)
                norm_stats(0, n)

            def b_norm(n, part):
                bb = lambda k: dve.wait_ge(v_b.sem, v_b.at(n, k))
                if part == 0:
                    dve.wait_ge(a_small.sem, a_small.at(n))
                    tt(lg_b[:], small[:, :, PROJ:PROJ + 4], all_tiles(bp_logit[:], 4), ALU.add).then_inc(v_b.sem, 1)
                    tt(proj[:], small[:, :, 0:PROJ], all_tiles(const("bp"), PROJ), ALU.add).then_inc(v_b.sem, 1)
                if part == 1:
                    bb(2)
                    tt(proj_sq[:], proj[:], proj[:], ALU.mult).then_inc(v_b.sem, 1)
                    bb(3)
                    red(proj_n2[:], proj_sq[:], AX.X, ALU.add).then_inc(v_b.sem, 1)
                    bb(4)
                    ts(proj_n2c[:], proj_n2[:], 1e-24, None, ALU.max).then_inc(v_b.sem, 1)

            def b_logits(n):
                bb = lambda k: dve.wait_ge(v_b.sem, v_b.at(n, k))
                dve.wait_ge(g_b.sem, g_b.at(n))
                tt(lg[:], lg_b[:], per_tile(proj_rn[:]), ALU.mult).then_inc(v_b.sem, 1)
                bb(6)
                red(lg_max[:], lg[:], AX.X, ALU.max).then_inc(v_b.sem, 1)
                bb(7)
                tt(lg_s[:], lg[:], per_tile(lg_max[:]), ALU.subtract).then_inc(v_b.sem, 1)

            def b_first(n):
                bb = lambda k: dve.wait_ge(v_b.sem, v_b.at(n, k))
                bb(8)
                stt(cand[:], lg_s[:], 0.0, all_tiles(const("order")), ALU.is_equal, ALU.mult).then_inc(v_b.sem, 1)
                bb(9)
                red(cand_max[:], cand[:], AX.X, ALU.max).then_inc(v_b.sem, 1)
                bb(10)
                tt(first[:], cand[:], per_tile(cand_max[:]), ALU.is_equal).then_inc(v_b.sem, 1)

            def b_weigh(n):
                bb = lambda k: dve.wait_ge(v_b.sem, v_b.at(n, k))
                dve.wait_ge(a_b.sem, a_b.at(n))
                red(lg_sum[:], lg_e[:], AX.X, ALU.add).then_inc(v_b.sem, 1)
                bb(12)
                nc.vector.reciprocal(lw_max[:], lg_sum[:]).then_inc(v_b.sem, 1)
                bb(13)
                tt(ret[:], first[:], per_tile(lw_max[:]), ALU.mult).then_inc(v_b.sem, 1)
                bb(14)
                at = 0
                for e, k in enumerate(RANKS):
                    tt(down_m[:, :, at:at + k], small[:, :, PROJ + 4 + at:PROJ + 4 + at + k],
                       ret[:, :, e:e + 1].broadcast_to([P, TILES, k]), ALU.mult).then_inc(v_down.sem, 1)
                    at += k
                dve.wait_ge(v_down.sem, v_down.at(n, len(RANKS)))
                high = down_x[:, :, 0:2, 0:RANK_SUM]
                nc.vector.tensor_copy(high.bitcast(F32R), down_m[:].unsqueeze(2).broadcast_to([P, TILES, 2, RANK_SUM])).then_inc(v_down.sem, 1)
                dve.wait_ge(v_down.sem, v_down.at(n, len(RANKS) + 1))
                tt(down_x[:, :, 2, 0:RANK_SUM], down_m[:], down_x[:, :, 0, 0:RANK_SUM], ALU.subtract).then_inc(v_down.sem, 1)

            def conv_tap(n, j):
                taps = const("taps")
                if j == 1:
                    dve.wait_ge(a_tap.sem, a_tap.at(n))
                else:
                    dve.wait_ge(v_conv.sem, v_conv.at(n, j - 1))
                stt(conv[:], vT[:, :, j:j + SEQ], taps[:, j:j + 1], conv[:], ALU.mult, ALU.add).then_inc(v_conv.sem, 1)

            def r_groups(r, part):
                rr = lambda k: dve.wait_ge(v_r.sem, v_r.at(r, k))
                flat = score[:].rearrange("p t e -> p (t e)")
                two = score[:].rearrange("p t (a b) -> p (t a) b", b=2)
                hh = pair_hi[:].rearrange("p (a b) -> p a b", b=2)
                ss = pair_sum[:].rearrange("p (a b) -> p a b", b=2)
                spread = [P, TILES, GROUPS, GROUPS]
                groups = lambda ap: ap.rearrange("p t i j -> p t (i j)")
                by_group = lambda ap: ap.rearrange("p t (g j) -> p (t g) j", g=GROUPS)
                if part == 0:
                    dve.wait_ge(a_ez.sem, a_ez.at(r))
                    ts(ez1[:], ez[:], 1.0, None, ALU.add).then_inc(v_r.sem, 1)
                if part == 1:
                    rr(1)
                    nc.vector.reciprocal(flat, ez1[:]).then_inc(v_r.sem, 1)
                if part == 2:
                    rr(2)
                    tt(pair_sum[:], two[:, :, 0], two[:, :, 1], ALU.add).then_inc(v_r.sem, 1)
                    tt(pair_hi[:], two[:, :, 0], two[:, :, 1], ALU.max).then_inc(v_r.sem, 1)
                if part == 3:
                    rr(3)
                    tt(inner[:], ss[:, :, 0], ss[:, :, 1], ALU.max).then_inc(v_r.sem, 1)
                    rr(4)
                    tt(cross[:], hh[:, :, 0], hh[:, :, 1], ALU.add).then_inc(v_r.sem, 1)
                if part == 4:
                    rr(6)
                    tt(gscore[:].rearrange("p t g -> p (t g)"), cross[:], inner[:], ALU.max).then_inc(v_r.sem, 1)
                    rr(7)
                    tt(g_diff[:], gscore[:].unsqueeze(2).broadcast_to(spread), gscore[:].unsqueeze(3).broadcast_to(spread),
                       ALU.subtract).then_inc(v_r.sem, 1)
                    rr(8)
                    stt(groups(g_tie[:]), groups(g_diff[:]), 0.0, all_tiles(const("before"), GROUPS * GROUPS),
                        ALU.is_equal, ALU.mult).then_inc(v_r.sem, 1)
                    rr(9)
                    stt(g_beat[:], g_diff[:], 0.0, g_tie[:], ALU.is_gt, ALU.add).then_inc(v_r.sem, 1)
                    rr(10)
                    red(g_rank[:], g_beat[:], AX.X, ALU.add).then_inc(v_r.sem, 1)
                    rr(11)
                    ts(penalty[:], g_rank[:], 1.5, -3.0, ALU.is_gt, ALU.mult).then_inc(v_r.sem, 1)
                    rr(12)
                    tt(by_group(masked[:]), by_group(score[:]),
                       penalty[:].rearrange("p t g -> p (t g)").unsqueeze(2).broadcast_to([P, TILES * GROUPS, EXPERTS // GROUPS]),
                       ALU.add).then_inc(v_r.sem, 1)

            def b_res(n):
                dve.wait_ge(p_up.sem, p_up.at(n))
                tt(res[1][:], x1[:], tiles(B1[:]), ALU.add).then_inc(v_res[1].sem, 1)
                norm_stats(1, n)

            def c_max(n):
                for s, b in ((0, B0), (1, B1)):
                    dve.wait_ge(p_s.sem, p_s.at(n, s + 1))
                    for i, (a, w) in enumerate(((0, P), (P, 2 * P))):
                        red(neg_max[:, 2 * s + i:2 * s + i + 1], b[:, a:a + w], AX.X, ALU.max, negate=True).then_inc(v_max.sem, 1)

            def c_res(n):
                dve.wait_ge(a_exp.sem, a_exp.at(n))
                nc.vector.reciprocal(row_inv[:], row_sum[:]).then_inc(v_rinv.sem, 1)
                dve.wait_ge(v_rinv.sem, v_rinv.at(n))
                dve.wait_ge(p_av.sem, p_av.at(n))
                dve.wait_ge(g_x2b.sem, g_x2b.at(n))
                for t in range(TILES):
                    stt(res[2][:, t, :], B1[:, t * P:(t + 1) * P], row_inv[:, t:t + 1], x2_b[:, t, :],
                        ALU.mult, ALU.add).then_inc(v_res[2].sem, 1)
                norm_stats(2, n)

            def r_combine(n):
                rr = lambda k: dve.wait_ge(v_r.sem, v_r.at(n, k))
                rr(R_MASKED)
                nc.vector.memset(n_above[:], 0.0)
                for t in range(TILES):
                    nc.vector.max(top8[:, t, :], masked[:, t, :]).then_inc(v_r.sem, 1)
                rr(R_TOP)
                fourth = top8[:, :, 3:4].broadcast_to([P, TILES, EXPERTS])
                flat = lambda ap: ap.rearrange("p t e -> p (t e)")
                tt(above[:], masked[:], fourth, ALU.is_gt).then_inc(v_r.sem, 1)
                tt(equal[:], masked[:], fourth, ALU.is_equal).then_inc(v_r.sem, 1)
                rr(R_TOP + 1)
                red(n_above[:], above[:], AX.X, ALU.add).then_inc(v_r.sem, 1)
                rr(R_TOP + 2)
                nc.vector.tensor_tensor_scan(flat(count[:]), const("carry"), flat(equal[:]), 0.0,
                                             ALU.mult, ALU.add).then_inc(v_r.sem, 1)
                rr(R_TOP + 4)
                tt(place[:], count[:], per_tile(n_above[:], EXPERTS), ALU.add).then_inc(v_r.sem, 1)
                rr(R_TOP + 5)
                stt(tied[:], place[:], 4.5, equal[:], ALU.is_lt, ALU.mult).then_inc(v_r.sem, 1)
                rr(R_TOP + 6)
                tt(chosen[:], tied[:], above[:], ALU.add).then_inc(v_r.sem, 1)
                rr(R_TOP + 7)
                tt(wsel[:], chosen[:], score[:], ALU.mult).then_inc(v_r.sem, 1)
                rr(R_TOP + 8)
                red(wsum[:], wsel[:], AX.X, ALU.add).then_inc(v_r.sem, 1)
                rr(R_TOP + 9)
                ts(wsum_e[:], wsum[:], 1e-6, None, ALU.add).then_inc(v_r.sem, 1)
                rr(R_TOP + 10)
                nc.vector.reciprocal(winv[:], wsum_e[:]).then_inc(v_r.sem, 1)
                rr(R_TOP + 11)
                tt(comb[:], wsel[:], per_tile(winv[:], EXPERTS), ALU.mult).then_inc(v_r.sem, 1)

            def d_gu(n, c):
                dve.wait_ge(a_silu.sem, a_silu.at(n, c + 1))
                dve.wait_ge(p_U.sem, p_U.at(n, c + 1))
                if c < CHUNKS:
                    tt(gu[:, c % 2], silu[:, c % 2], UB[:], ALU.mult).then_inc(v_gu.sem, 1)
                else:
                    dve.wait_ge(p_w2.sem, p_w2.at(n, c - 1))
                    tt(hid[:, c % 2], silu[:, c % 2], UB[:], ALU.mult).then_inc(v_gu.sem, 1)

            def d_hid(n, c):
                dve.wait_ge(v_gu.sem, v_gu.at(n, c + 1))
                dve.wait_ge(p_C.sem, p_C.at(n, c + 1))
                if c > 1 or started(n):
                    dve.wait_ge(p_w2.sem, p_w2.at(n, max(c - 1, 0)))
                tt(hid[:, c % 2], gu[:, c % 2], CB[:], ALU.mult).then_inc(v_hid.sem, 1)

            def d_res(n, odd):
                if started(n):
                    dve.wait_ge(g_cent.sem, g_cent.at(n - 1))
                dve.wait_ge(p_yT.sem, p_yT.at(n))
                tt(res[3][:], x3[odd][:], tiles(YB[:]), ALU.add).then_inc(v_res[3].sem, 1)
                norm_stats(3, n)

            def turn(i, odd):
                a, b, c, d, e = live(i), live(i - 1), live(i - 2), live(i - 3), live(i - 4)
                if d: d_gu(i - 3, 0)
                if c: c_max(i - 2)
                if d: d_hid(i - 3, 0)
                if e: d_res(i - 4, odd)
                if d: d_gu(i - 3, 1)
                if d: d_hid(i - 3, 1)
                if b: a_layer_norm(i - 1)
                if d: d_gu(i - 3, 2)
                if d: d_hid(i - 3, 2)
                if a: a_rope(i)
                if c: c_res(i - 2)
                if d: d_gu(i - 3, 3)
                if b: b_norm(i - 1, 0)
                if d: d_hid(i - 3, 3)
                if b: b_norm(i - 1, 1)
                if d: d_gu(i - 3, 4)
                if b: b_logits(i - 1)
                if d: d_hid(i - 3, 4)
                if a: a_kv(i)
                if b: b_first(i - 1)
                if b: b_weigh(i - 1)
                if a: conv_tap(i, 1)
                if d: d_gu(i - 3, 5)
                if a: conv_tap(i, 2)
                if d: d_hid(i - 3, 5)
                if a: conv_tap(i, 3)
                if c: r_groups(i - 2, 0)
                if a: conv_tap(i, 4)
                if c: r_groups(i - 2, 1)
                if d: d_gu(i - 3, 6)
                if c: r_groups(i - 2, 2)
                if a: a_den(i)
                if b: b_res(i - 1)
                if c: r_groups(i - 2, 3)
                if d: d_hid(i - 3, 6)
                if c: r_groups(i - 2, 4)
                if d: d_gu(i - 3, 7)
                if d: d_hid(i - 3, 7)
                if a: a_att(i)
                if d: d_gu(i - 3, 8)
                if a: a_gate(i)
                if c: r_combine(i - 2)
                if a: a_res(i, odd)

            for i in range(LEAD):
                if i == 1:
                    split_late()
                turn(i, i % 2)
            with dve.Fori(0, loops) as k:
                turn(2 * k + LEAD, 0)
                turn(2 * k + LEAD + 1, 1)
            for i in range(blocks, turns):
                turn(i, i % 2)

        @block.gpsimd
        def _(pool):
            tt = nc.gpsimd.tensor_tensor
            pool.wait_ge(k_in.sem, 16)
            nc.gpsimd.memset(comb_b[:], 0.0).then_inc(setup_g.sem, 1)
            nc.gpsimd.memset(v_one[:, :, P:P + 1], 1.0).then_inc(setup_g.sem, 1)
            pool.wait_ge(setup_v.sem, 5)
            tt(sim_rn[:], sim_n2[:], const("neg_half", PROJ), ALU.pow).then_inc(setup_g.sem, 1)
            nc.gpsimd.memset(vT[:, :, 0:2], 0.0).then_inc(setup_g.sem, 1)
            nc.gpsimd.memset(vT[:, :, SEQ + 2:SEQ + 4], 0.0).then_inc(setup_g.sem, 1)
            nc.gpsimd.memset(conv[:], 0.0).then_inc(setup_g.sem, 1)

            def a_rope(n):
                for h in range(2):
                    pool.wait_ge(v_rope.sem, v_rope.at(n, 3 * h + 3))
                    tt(qk[:, 2 * h:2 * h + 2, :].rearrange("p t d -> p (t d)"), rope_c[:, h], rope_s[:, h],
                       ALU.add).then_inc(g_qk.sem, 1)

            def split3(n, src, rest, parts, sem, w):
                zeros = const("zero")[:, 0:TILES * w].rearrange("p (t c) -> p t c", t=TILES)
                tt(parts[:, :, 0, :], src[:], zeros, ALU.add).then_inc(sem.sem, 1)
                pool.wait_ge(sem.sem, sem.at(n, 1))
                tt(rest[:], src[:], parts[:, :, 0, :], ALU.subtract).then_inc(sem.sem, 1)
                pool.wait_ge(sem.sem, sem.at(n, 2))
                tt(parts[:, :, 1, :], rest[:], zeros, ALU.add).then_inc(sem.sem, 1)
                pool.wait_ge(sem.sem, sem.at(n, 3))
                tt(parts[:, :, 2, :], rest[:], parts[:, :, 1, :], ALU.subtract).then_inc(sem.sem, 1)

            def a_rd(n):
                pool.wait_ge(v_rden.sem, v_rden.at(n))
                heads = rden[:].rearrange("p t h -> p (t h)").unsqueeze(2).broadcast_to([P, TILES * HEADS, HD])
                ones = const("ones")[:, 0:HD].unsqueeze(1).broadcast_to([P, TILES * HEADS, HD])
                tt(rden_x[:].rearrange("p t (h d) -> p (t h) d", d=HD), heads, ones, ALU.mult).then_inc(g_rd.sem, 1)

            def a_mix(n):
                pool.wait_ge(v_att.sem, v_att.at(n))
                pool.wait_ge(v_conv.sem, v_conv.at(n))
                tt(mixT[:], attT[:], conv[:].rearrange("p s l -> p (s l)"), ALU.add).then_inc(g_mix.sem, 1)

            def ln_of(k, n):
                pool.wait_ge(v_st[k].sem, v_st[k].at(n))
                count, m, st = [0], moment[k], stats[k]

                def put(out, in0, in1, op, chained=True):
                    tt(out, in0, in1, op).then_inc(g_ln[k].sem, 1)
                    count[0] += 1
                    if chained:
                        pool.wait_ge(g_ln[k].sem, g_ln[k].at(n, count[0]))

                put(m[:, 0], st[:, :, 1], st[:, :, 4], ALU.add, False)
                put(m[:, 1], st[:, :, 1], st[:, :, 4], ALU.subtract, False)
                put(m[:, 2], st[:, :, 2], st[:, :, 5], ALU.add)
                put(mean[k][:], m[:, 0], const("neg_half" if k == 1 else "half"), ALU.mult, False)
                put(m[:, 3], m[:, 1], m[:, 1], ALU.mult, False)
                put(m[:, 4], m[:, 2], const("inv_p"), ALU.mult)
                put(m[:, 5], m[:, 3], const("quarter"), ALU.mult, False)
                put(m[:, 6], m[:, 4], const("eps"), ALU.add)
                put(m[:, 7], m[:, 5], m[:, 6], ALU.add)
                put(rstd[k][:], m[:, 7], const("neg_half"), ALU.pow, k == 1)
                if k == 1:
                    put(shift[:], mean[k][:], rstd[k][:], ALU.mult, False)

            def b_norm(n):
                pool.wait_ge(v_b.sem, v_b.at(n, B_NORM2))
                tt(proj_rn[:], proj_n2c[:], const("neg_half"), ALU.pow).then_inc(g_b.sem, 1)

            def r_split(n):
                pool.wait_ge(v_r.sem, v_r.at(n))
                split3(n, comb, comb_r, comb_b[:, :, 0:3], g_c, EXPERTS)

            def x2_bias(n):
                pool.wait_ge(a_x2.sem, a_x2.at(n))
                tt(x2_b[:], x2[:], const("bcv").unsqueeze(1).broadcast_to([P, TILES, P]), ALU.add).then_inc(g_x2b.sem, 1)

            def x0_lo(n):
                pool.wait_ge(a_x0h.sem, a_x0h.at(n))
                pool.wait_ge(a_xT[0].sem, a_xT[0].at(n))
                tt(x0T_lo[:], xT[0][:], x0T_hi[:].bitcast(F32), ALU.subtract).then_inc(g_x0l.sem, 1)

            def x3_lo(n, odd):
                pool.wait_ge(a_xT[3].sem, a_xT[3].at(n))
                pool.wait_ge(a_x3h.sem, a_x3h.at(n))
                tt(x3T_lo[odd][:], xT[3][:], x3T_hi[odd][:].bitcast(F32), ALU.subtract).then_inc(g_x3l.sem, 1)

            def c_norm(n, odd):
                pool.wait_ge(g_ln[2].sem, g_ln[2].at(n))
                tt(x3[odd][:], res[2][:], mean[2][:].unsqueeze(2).broadcast_to([P, TILES, P]), ALU.subtract).then_inc(g_x3.sem, 1)
                pool.wait_ge(g_x3.sem, g_x3.at(n, 1))
                tt(x3[odd][:], x3[odd][:], rstd[2][:].unsqueeze(2).broadcast_to([P, TILES, P]), ALU.mult).then_inc(g_x3.sem, 1)

            def e_norm(n):
                pool.wait_ge(g_ln[3].sem, g_ln[3].at(n))
                tt(centered[:], res[3][:], mean[3][:].unsqueeze(2).broadcast_to([P, TILES, P]), ALU.subtract).then_inc(g_cent.sem, 1)
                pool.wait_ge(g_cent.sem, g_cent.at(n))
                if started(n):
                    pool.wait_ge(x_st.sem, x_st.at(n - 1))
                tt(x4[:], centered[:], rstd[3][:].unsqueeze(2).broadcast_to([P, TILES, P]), ALU.mult).then_inc(g_x4.sem, 1)

            def turn(i, odd):
                a, b, c, d, e = live(i), live(i - 1), live(i - 2), live(i - 3), live(i - 4)
                if a: x0_lo(i)
                if e: ln_of(3, i - 4)
                if a: a_rope(i)
                if c: ln_of(2, i - 2)
                if b: b_norm(i - 1)
                if c: c_norm(i - 2, odd)
                if e: e_norm(i - 4)
                if c: x3_lo(i - 2, odd)
                if a: a_rd(i)
                if b: ln_of(1, i - 1)
                if a: a_mix(i)
                if c: r_split(i - 2)
                if b: x2_bias(i - 1)
                if a: ln_of(0, i)

            for i in range(LEAD):
                turn(i, i % 2)
            with pool.Fori(0, loops) as k:
                turn(2 * k + LEAD, 0)
                turn(2 * k + LEAD + 1, 1)
            for i in range(blocks, turns):
                turn(i, i % 2)


def _constants():
    c = {}
    inv_freq = (1.0 / np.float32(10000.0) ** (np.arange(0, HD, 2, dtype=np.float32) / np.float32(HD))).astype(np.float32)
    freqs = np.arange(SEQ, dtype=np.float32)[:, None] * inv_freq[None, :]
    emb = np.concatenate([freqs, freqs], axis=-1)
    sin, cos = np.sin(emb).astype(np.float32), np.cos(emb).astype(np.float32)
    sin = np.concatenate([-sin[:, :HD // 2], sin[:, HD // 2:]], axis=-1)
    spread = lambda t: np.tile(t.reshape(2, P, 1, HD), (1, 1, 2 * HEADS, 1)).transpose(1, 0, 2, 3).reshape(P, BLOCK)
    c["cos"], c["sin"] = spread(cos), spread(sin)
    d = np.arange(P)
    c["hmask"] = (d[:, None] // HD == d[None, :] // HD) * np.float32(A_SCALE)
    c["hmask8"] = (d[:, None] // HD == np.arange(HEADS)[None, :]) * np.float32(A_SCALE)
    c["ident"] = np.eye(P)
    c["causal"] = np.where(d[None, :] > d[:, None], np.float32(MASKED), 0.0)
    c["order"] = np.tile(np.arange(4, 0, -1), (P, 1))
    g = np.arange(GROUPS)
    c["before"] = np.tile((g[None, :] < g[:, None]).reshape(1, -1), (P, 1))
    c["ones"] = np.ones((P, P))
    f = np.arange(CHUNKS * P)
    c["sel_exp"] = np.tile(np.arange(EXPERTS), 3)[:, None] == f[None, :] // EF
    c["carry"] = np.tile(np.arange(TILES * EXPERTS) % EXPERTS != 0, (P, 1))
    for name, value in (("zero", 0.0), ("half", 0.5), ("neg_half", -0.5), ("quarter", 0.25), ("inv_p", 1.0 / P),
                        ("eps", EPS)):
        lo, up = CONST_COLS[name]
        c[name] = np.full((P, up - lo), value)
    return c


def _fill(width, table, parts):
    out = np.zeros((P, width), np.float32)
    for name, a in parts.items():
        lo, up = table[name]
        out[:a.shape[0], lo:lo + a.shape[1]] = a
    return out


def kernel(**inputs):
    import concourse.bacc as _bacc
    from concourse.bass_utils import run_bass_kernel_spmd as _run

    w = {k: np.asarray(v) for k, v in inputs.items()}
    x = np.ascontiguousarray(w["L0_attn_hidden_states"])
    ffn = lambda a: w["L0_ffn_" + a]
    moe = lambda a: w["L1_ffn_" + a]
    hidden = lambda e, s: np.concatenate([moe(e).reshape(EXPERTS * EF, P), moe(s)], axis=0).T
    down = np.concatenate([moe("w2_e").transpose(0, 2, 1).reshape(EXPERTS * EF, P), moe("w2_s").T], axis=0)
    rows = lambda a: np.repeat(a.reshape(1, -1), P, axis=0)
    up = np.zeros((3, SUB, P), np.float32)
    up[:, 0:RANK_SUM] = np.concatenate([ffn(f"Wu{i}").T for i in range(4)], axis=0)
    up = up.reshape(3 * SUB, P)
    weight = {
        "qk": np.concatenate([w["L0_attn_Wq"], w["L0_attn_Wk"]], axis=0).T, "v": w["L0_attn_Wv"].T, "g": w["L0_attn_Wg"].T,
        "base": ffn("W").T, "proj": ffn("Wp").T, "down": np.concatenate([ffn(f"Wd{i}") for i in range(4)], axis=0).T,
        "cq": w["L1_attn_W"][:, 0:P], "ck": w["L1_attn_W"][:, P:2 * P], "cv": w["L1_attn_W"][:, 2 * P:3 * P],
        "gate": moe("w_gate").T, "w1": hidden("w1_e", "w1_s"), "w3": hidden("w3_e", "w3_s"),
    }
    whole = _constants()
    whole.update({
        "wo": w["L0_attn_Wo"].T, "w2": down.reshape(ALLCH, P, P).transpose(1, 0, 2).reshape(P, ALLCH * P),
        "taps": w["L0_attn_lepe_w"].reshape(P, TAPS), "tapb": w["L0_attn_lepe_b"].reshape(P, 1),
        "bp": rows(ffn("bp")), "bcq": w["L1_attn_b"][0:P].reshape(P, 1), "bck": w["L1_attn_b"][P:2 * P].reshape(P, 1),
        "bcv": rows(w["L1_attn_b"][2 * P:3 * P]), "temp": rows(ffn("temp")), "wp": ffn("Wp"), "sim": ffn("sim"),
        "bprep": np.repeat(ffn("bp").reshape(PROJ, 1), P, axis=1),
        "up": up,
    })
    arrays = {
        "x": x.reshape(-1, P),
        "w": _fill(N_WEIGHT, WEIGHT_COLS, weight),
        "w_whole": _fill(N_CONST, CONST_COLS, whole),
    }
    nc = _bacc.Bacc("TRN2", target_bir_lowering=False, num_devices=1)
    args = [nc.dram_tensor(name, a.shape, F32, kind="ExternalInput").ap() for name, a in arrays.items()]
    out = nc.dram_tensor("out", arrays["x"].shape, F32, kind="ExternalOutput").ap()
    build(nc, *args, out)
    r = _run(nc, [arrays], core_ids=[0])
    return r.results[0]["out"].reshape(x.shape)
```
